# Optimizing a Trainium2 kernel written in Bass

```python
import numpy as np
import jax
import jax.numpy as jnp

def _softmax(x, axis=-1):
    return jax.nn.softmax(x, axis=axis)

def _gelu(x):
    return jax.nn.gelu(x, approximate=True)

def _silu(x):
    return jax.nn.silu(x)

def _sigmoid(x):
    return jax.nn.sigmoid(x)

def _layernorm(x, axis=-1, eps=1e-05):
    m = jnp.mean(x, axis=axis, keepdims=True)
    v = jnp.var(x, axis=axis, keepdims=True)
    return (x - m) / jnp.sqrt(v + eps)

def _scatter_add(tgt, idx, src, axis=0):
    return tgt.at[idx].add(src)

def _segment_sum(src, seg, n):
    return jax.ops.segment_sum(src, seg, n)
kernel_name = 'mk_prb_d1_jaxref_r8_426401'

def setup_inputs(seed: int=0):
    np.random.seed(seed)
    _w = jnp.asarray

    def _L0_attn_setup():
        import jax, jax.numpy as jnp
        import numpy as np
        B, S, D, L = (4, 256, 128, 4)

        def _retention(x, wkqv):
            d = x.shape[-1]
            k, q, v = jnp.split(x @ wkqv, 3, axis=-1)
            qkt = jnp.einsum('bid,bjd->bij', q, k) / jnp.sqrt(jnp.float32(d))
            s = x.shape[1]
            row_norm = 1.0 + jnp.sqrt(jnp.arange(s, dtype=x.dtype))[None, :, None]
            r = jnp.tril(qkt) / row_norm
            denom = jnp.clip(jnp.abs(r.sum(-1, keepdims=True)), 1.0, None)
            r = r / denom
            return jnp.einsum('bij,bjd->bid', r, v)

        def _groupnorm1(y, g, b, eps=1e-05):
            mu = y.mean(axis=(1, 2), keepdims=True)
            var = y.var(axis=(1, 2), keepdims=True)
            return (y - mu) / jnp.sqrt(var + eps) * g + b

        def _layernorm(y, g, b, eps=1e-05):
            mu = y.mean(-1, keepdims=True)
            var = y.var(-1, keepdims=True)
            return (y - mu) / jnp.sqrt(var + eps) * g + b
        key = jax.random.key(seed)
        ks = jax.random.split(key, 6)
        w = lambda k, shape: jax.random.normal(k, shape, jnp.float32) * 0.02
        return {'x': jax.random.normal(ks[0], (B, S, D), jnp.float32), 'Wkqv': w(ks[1], (L, D, 3 * D)), 'Wm1': w(ks[2], (L, D, 2 * D)), 'bm1': jnp.zeros((L, 2 * D), jnp.float32), 'Wm2': w(ks[3], (L, D, D)), 'bm2': jnp.zeros((L, D), jnp.float32), 'gn_g': jnp.ones((L, D), jnp.float32), 'gn_b': jnp.zeros((L, D), jnp.float32), 'Wf1': w(ks[4], (L, D, 2 * D)), 'bf1': jnp.zeros((L, 2 * D), jnp.float32), 'Wf2': w(ks[5], (L, 2 * D, D)), 'bf2': jnp.zeros((L, D), jnp.float32), 'ln_g': jnp.ones((L, D), jnp.float32), 'ln_b': jnp.zeros((L, D), jnp.float32)}
    _L0_attn_in = _L0_attn_setup()

    def _L0_ffn_setup():
        import jax, jax.numpy as jnp
        import numpy as np
        B, S, D_IN, D_OUT, E, K = (2, 256, 128, 128, 8, 2)
        key = jax.random.key(seed)
        k1, k2, k3, k4 = jax.random.split(key, 4)
        scale = 1.0 / np.sqrt(D_IN)
        return {'inputs': jax.random.normal(k1, (B, S, D_IN), dtype=jnp.float32), 'Wg': jax.random.normal(k2, (E, D_IN), dtype=jnp.float32) * scale, 'We': jax.random.normal(k3, (E, D_OUT, D_IN), dtype=jnp.float32) * scale, 'be': jax.random.normal(k4, (E, D_OUT), dtype=jnp.float32) * scale}
    _L0_ffn_in = _L0_ffn_setup()
    _d = {'L0_attn_x': _L0_attn_in['x'], 'L0_attn_Wkqv': _L0_attn_in['Wkqv'], 'L0_attn_Wm1': _L0_attn_in['Wm1'], 'L0_attn_bm1': _L0_attn_in['bm1'], 'L0_attn_Wm2': _L0_attn_in['Wm2'], 'L0_attn_bm2': _L0_attn_in['bm2'], 'L0_attn_gn_g': _L0_attn_in['gn_g'], 'L0_attn_gn_b': _L0_attn_in['gn_b'], 'L0_attn_Wf1': _L0_attn_in['Wf1'], 'L0_attn_bf1': _L0_attn_in['bf1'], 'L0_attn_Wf2': _L0_attn_in['Wf2'], 'L0_attn_bf2': _L0_attn_in['bf2'], 'L0_attn_ln_g': _L0_attn_in['ln_g'], 'L0_attn_ln_b': _L0_attn_in['ln_b'], 'L0_ffn_Wg': _L0_ffn_in['Wg'], 'L0_ffn_We': _L0_ffn_in['We'], 'L0_ffn_be': _L0_ffn_in['be']}
    _x0 = _d['L0_attn_x']
    _d['L0_attn_x'] = jax.random.normal(jax.random.fold_in(jax.random.key(seed), 1), (8, 512, 128), dtype=_x0.dtype)
    del _x0
    return _d

def reference(L0_attn_x, L0_attn_Wkqv, L0_attn_Wm1, L0_attn_bm1, L0_attn_Wm2, L0_attn_bm2, L0_attn_gn_g, L0_attn_gn_b, L0_attn_Wf1, L0_attn_bf1, L0_attn_Wf2, L0_attn_bf2, L0_attn_ln_g, L0_attn_ln_b, L0_ffn_Wg, L0_ffn_We, L0_ffn_be):

    def _L0_attn_ref(x, Wkqv, Wm1, bm1, Wm2, bm2, gn_g, gn_b, Wf1, bf1, Wf2, bf2, ln_g, ln_b):
        import jax, jax.numpy as jnp
        import numpy as np
        B, S, D, L = (4, 256, 128, 4)

        def _retention(x, wkqv):
            d = x.shape[-1]
            k, q, v = jnp.split(x @ wkqv, 3, axis=-1)
            qkt = jnp.einsum('bid,bjd->bij', q, k) / jnp.sqrt(jnp.float32(d))
            s = x.shape[1]
            row_norm = 1.0 + jnp.sqrt(jnp.arange(s, dtype=x.dtype))[None, :, None]
            r = jnp.tril(qkt) / row_norm
            denom = jnp.clip(jnp.abs(r.sum(-1, keepdims=True)), 1.0, None)
            r = r / denom
            return jnp.einsum('bij,bjd->bid', r, v)

        def _groupnorm1(y, g, b, eps=1e-05):
            mu = y.mean(axis=(1, 2), keepdims=True)
            var = y.var(axis=(1, 2), keepdims=True)
            return (y - mu) / jnp.sqrt(var + eps) * g + b

        def _layernorm(y, g, b, eps=1e-05):
            mu = y.mean(-1, keepdims=True)
            var = y.var(-1, keepdims=True)
            return (y - mu) / jnp.sqrt(var + eps) * g + b

        def block(h, p):
            wk, w1, b1, w2, b2, gg, gb, wf1, bf1_, wf2, bf2_, lg, lb = p
            r = _retention(h, wk)
            m = r @ w1 + b1
            a, gate = jnp.split(m, 2, axis=-1)
            m = a * jax.nn.silu(gate) @ w2 + b2
            m = _groupnorm1(m, gg, gb)
            y = m + h
            f = jax.nn.gelu(y @ wf1 + bf1_, approximate=False) @ wf2 + bf2_
            return (_layernorm(f + y, lg, lb), None)
        params = (Wkqv, Wm1, bm1, Wm2, bm2, gn_g, gn_b, Wf1, bf1, Wf2, bf2, ln_g, ln_b)
        out, _ = jax.lax.scan(block, x, params)
        return out

    def _L0_ffn_ref(inputs, Wg, We, be):
        import jax, jax.numpy as jnp
        import numpy as np
        B, S, D_IN, D_OUT, E, K = (2, 256, 128, 128, 8, 2)
        logits = jnp.einsum('bsd,ed->bse', inputs, Wg)
        topw, sel = jax.lax.top_k(logits, K)
        topw = jax.nn.softmax(topw.astype(jnp.float32), axis=-1).astype(inputs.dtype)
        cw = jnp.sum(jax.nn.one_hot(sel, E, dtype=topw.dtype) * topw[..., None], axis=-2)
        y = jnp.einsum('bsd,eod->bseo', inputs, We) + be
        return jnp.einsum('bseo,bse->bso', y, cw)
    x = L0_attn_x
    xn = _layernorm(x, axis=-1)
    x = x + _L0_attn_ref(xn, L0_attn_Wkqv, L0_attn_Wm1, L0_attn_bm1, L0_attn_Wm2, L0_attn_bm2, L0_attn_gn_g, L0_attn_gn_b, L0_attn_Wf1, L0_attn_bf1, L0_attn_Wf2, L0_attn_bf2, L0_attn_ln_g, L0_attn_ln_b) + _L0_ffn_ref(xn, L0_ffn_Wg, L0_ffn_We, L0_ffn_be)
    return x

_drawn_inputs = setup_inputs


def setup_inputs(seed=0):
    import zlib

    import numpy as np

    out = dict(_drawn_inputs(seed))
    spreads = {'L0_attn_bm1': (0.0, 0.8),
     'L0_attn_bm2': (0.0, 0.8),
     'L0_attn_gn_g': (1.0, 0.2),
     'L0_attn_gn_b': (0.0, 0.1),
     'L0_attn_bf1': (0.0, 0.8),
     'L0_attn_bf2': (0.0, 0.1),
     'L0_attn_ln_g': (1.0, 0.2),
     'L0_attn_ln_b': (0.0, 0.1)}
    factors = {'L0_attn_Wkqv': 8.0, 'L0_attn_Wm1': 8.0, 'L0_attn_Wm2': 8.0}
    for name, (base, spread) in spreads.items():
        noise = np.random.default_rng([zlib.crc32(name.encode()), seed]).standard_normal(out[name].shape)
        drawn = base * np.exp(spread * noise) if base else spread * noise
        out[name] = jnp.asarray(drawn.astype(out[name].dtype))
    for name, factor in factors.items():
        out[name] = (out[name] * factor).astype(out[name].dtype)
    return out
```

```python
from contextlib import ExitStack

import concourse.bass as bass
from concourse import mybir

F32 = mybir.dt.float32
ALU = mybir.AluOpType
ACT = mybir.ActivationFunctionType
AX = mybir.AxisListType

P = 128
GROUP = 4
EPS = 1e-5
AUG = P + 2

B1A, B1G, HALF_B1G, B2, GN_G, GN_B, BF1A, BF1B, BF2, LN_G, LN_B = range(11)
MIX, FEED, FINISH = slice(B1A, GN_G), slice(GN_G, LN_G), slice(LN_G, LN_B + 1)


def retention_moe(nc, x, Wkqv, Wm1, bm1, Wm2, bm2, gn_g, gn_b, Wf1, bf1, Wf2, bf2, ln_g, ln_b,
                  Wg, We, be, constants, out):
    NB, S, D = x.shape
    L = Wkqv.shape[0]
    E = Wg.shape[0]
    C = S // P
    NG = NB // GROUP
    ITEMS = GROUP * L
    CE = C * E
    CHUNKS = GROUP * C
    HALF = E // 2
    assert D == P and C == 4

    ctx = ExitStack()
    with ctx:
        def sb(name, *shape):
            return ctx.enter_context(nc.sbuf_tensor(name, list(shape), F32))

        def bank(name):
            return ctx.enter_context(nc.psum_tensor(name, [P, 512], F32))

        def sem(name):
            return ctx.enter_context(nc.semaphore(name))

        const = sb("const", P, 2 * P + C + E * E)
        ident, causal = const[:, 0:P], const[:, P:2 * P]
        row_norm = const[:, 2 * P:2 * P + C]
        norms = row_norm.rearrange("p (b c) -> p b c", b=2)
        earlier = const[:, 2 * P + C:]
        mean_of = sb("mean_of", P, P)
        minus_half = sb("minus_half", P, C)
        kqv_raw = sb("kqv_raw", P, L, 3 * D)
        wm1_raw = sb("wm1_raw", P, L, 2 * D)
        wm2_raw = sb("wm2_raw", P, L, D)
        wf1_raw = sb("wf1_raw", P, L, 2 * D)
        wf2_raw = sb("wf2_raw", P, L, 2, D)
        kqv_t = sb("kqv_t", P, 3 * D)
        a_all = sb("a_all", P, L, D)
        b_all = sb("b_all", P, L, 2 * D)
        rows = sb("rows", 10 * L, D)
        params = sb("params", P, 11, L)
        ln_bc = sb("ln_bc", P, 2, L, D)
        gate_rows = sb("gate_rows", E, D)
        gate_w = sb("gate_w", P, E)
        expert_rows = sb("expert_rows", P, E, D)
        expert_w = sb("expert_w", P, E, D)
        expert_b = sb("expert_b", CE, C, D)

        a_w = sb("a_w", P, D)
        b_w = sb("b_w", P, 2 * D)
        w2_w = sb("w2_w", P, D)
        ln_w = sb("ln_w", P, 2, D)
        f1_w = sb("f1_w", P, 2 * D)
        f2_w = sb("f2_w", P, 2, D)
        mix_p = sb("mix_p", P, 4)
        feed_p = sb("feed_p", P, 5)
        finish_p = sb("finish_p", P, 2)

        x_in = sb("x_in", P, GROUP, C, D)
        ht = sb("ht", P, GROUP, S)
        ha = sb("ha", P, GROUP, C, AUG)
        xnt = sb("xnt", P, GROUP, S)
        result = sb("result", P, GROUP, C, D)

        gt = sb("gt", P, S)
        past = sb("past", P, C - 1, AUG)
        scores = sb("scores", P, S)
        den = sb("den", P, 3, 2, 2)
        o_tok = sb("o_tok", P, C, D)
        ot = sb("ot", P, S)
        tanh_g = sb("tanh_g", P, S)
        a_in = sb("a_in", P, S)
        gated = sb("gated", P, S)
        mixed = sb("mixed", P, S)
        gn_st = sb("gn_st", P, 6)
        gn_mv = sb("gn_mv", P, 2)
        gn_m = sb("gn_m", P, 1)
        gn_d = sb("gn_d", P, 1)
        gn_p = sb("gn_p", P, 1)
        gn_b2 = sb("gn_b2", P, 1)
        gn_v = sb("gn_v", P, 1)
        gn_r = sb("gn_r", P, 1)
        gn_s = sb("gn_s", P, 1)
        gn_c = sb("gn_c", P, 1)
        up_bias = sb("up_bias", P, 2)
        z_bias = sb("z_bias", P, 1)
        y = sb("y", P, 2, S)
        gelu = sb("gelu", P, 2, S)
        zt = sb("zt", P, S)
        ln_stats = sb("ln_stats", P, C, 6)
        ln_mv = sb("ln_mv", P, C, 2)
        ln_var = sb("ln_var", P, C)
        ln_rstd = sb("ln_rstd", P, C)
        norm = sb("norm", P, C, D)
        scaled = sb("scaled", P, C, D)

        in_st = sb("in_st", P, GROUP, C, 6)
        in_mv = sb("in_mv", P, GROUP, C, 2)
        in_v = sb("in_v", P, GROUP, C)
        in_r = sb("in_r", P, GROUP, C)
        half_sum = sb("half_sum", P, 2, D)
        logits = sb("logits", P, CHUNKS, E)
        top = sb("top", P, CHUNKS)
        beats = sb("beats", P, CHUNKS, E, E)
        ties = sb("ties", P, CHUNKS, E, E)
        rank = sb("rank", P, CHUNKS, E)
        expo = sb("expo", P, CHUNKS, E)
        share = sb("share", P, CHUNKS, E)
        total = sb("total", P, CHUNKS)
        route = sb("route", P, CHUNKS, E)
        route_t = sb("route_t", CE, GROUP, P)

        X1, X2, Y1, Y2, Z1, Z2 = (bank(b) for b in ("X1", "X2", "Y1", "Y2", "Z1", "Z2"))
        O = ctx.enter_context(nc.psum_tensor("O", [P, 2, 512], F32))
        X3, M1 = O[:, 0, :], O[:, 1, :]
        o_sums = O[:, :, 0:2 * AUG].rearrange("p b (c a) -> p b c a", c=2)
        expert_banks = ((X2, X3), (M1, Y1))

        def several(kind, names):
            return [kind(name) for name in names.split()]

        consts_in, kqv_in, wm1_in, w_in, rows_in, gate_in, bc_in, ones_set = several(
            sem, "consts_in kqv_in wm1_in w_in rows_in gate_in bc_in ones_set")
        turned, turned_set, folded, folded_set, params_t, params_set, gate_t, gate_set, half_set = several(
            sem, "turned turned_set folded folded_set params_t params_set gate_t gate_set half_set")
        x_loaded, stored, in_stats = ([sem(f"{name}_{k}") for k in range(GROUP)]
                                      for name in ("x_loaded", "stored", "in_stats"))
        in_aggr, in_var, in_rstd, xnt_set = several(
            sem, "in_aggr in_var in_rstd xnt_set")
        logits_done, logits_set, route_turned, route_t_set, bias_done, bias_set = several(
            sem, "logits_done logits_set route_turned route_t_set bias_done bias_set")
        top_set, less_top, expo_set, beats_set, ties_set, ranks_set, rank_set, share_set, total_set, inverse_set, route_set = several(
            sem, "top_set less_top expo_set beats_set ties_set ranks_set rank_set share_set total_set inverse_set route_set")
        experts_done, moe_set = sem("experts_done"), sem("moe_set")
        first_sum = [sem(f"first_sum{j}") for j in range(HALF)]
        later_sum = [sem(f"later_sum{j}") for j in range(HALF)]
        g_done, gram_done, scores_done, o_done = several(sem, "g_done gram_done scores_done o_done")
        gt_set, past_one, past_two, past_set, scores_set = several(sem, "gt_set past_one past_two past_set scores_set")
        den_one, den_set, inv_set, o_set = several(sem, "den_one den_set inv_set o_set")
        ot_done, ot_set, gate_done, a_done, tanh_set, a_set, gated_set, mixed_set, mixed_done = several(
            sem, "ot_done ot_set gate_done a_done tanh_set a_set gated_set mixed_set mixed_done")
        gn_stats, gn_aggr, gn_means, gn_mean, gn_dev, gn_parts, gn_var, gn_veps, gn_rstd, gn_scale, gn_coef = several(
            sem, "gn_stats gn_aggr gn_means gn_mean gn_dev gn_parts gn_var gn_veps gn_rstd gn_scale gn_coef")
        c_done, c_set, y_set, f1a_done, f1b_done, gelu_a, gelu_b, f2_done, z_set = several(
            sem, "c_done c_set y_set f1a_done f1b_done gelu_a gelu_b f2_done z_set")
        z_turned, ln_stats_set, ln_aggr, ln_veps, ln_rs, norm_set, h_turned, ht_set, scaled_set, ha_set = several(
            sem, "z_turned ln_stats_set ln_aggr ln_veps ln_rs norm_set h_turned ht_set scaled_set ha_set")
        a_loaded, mix_loaded, feed_loaded, finish_loaded = several(
            sem, "a_loaded mix_loaded feed_loaded finish_loaded")
        out_set, result_set = several(sem, "out_set result_set")

        def nth(g, k):
            return GROUP * g + k + 1

        class Item:

            def __init__(self, n, layer, layers, count):
                self.n, self.k, self.layer, self.layers, self.count = n, n % GROUP, layer, layers, count

            last = property(lambda self: self.count(self.n))
            now = property(lambda self: self.count(self.n + 1))
            next = property(lambda self: self.count(self.n + 1 + GROUP))

        def run_slots(eng, g, slot):
            base = eng.snap(ITEMS * g)

            def slots(numbers, turn=None):
                counts = {}

                def count(items):
                    if items not in counts:
                        before = base if turn is None else base + GROUP * turn
                        counts[items] = eng.snap(before + items)
                    return counts[items]

                def at(j):
                    if turn is None and not 0 <= j < ITEMS:
                        return None
                    layer = j // GROUP if turn is None else turn + j // GROUP
                    return Item(j, layer, L * g + layer + 1, count)

                for n in numbers:
                    slot(n, at, g)

            slots(range(3))
            with eng.Fori(0, L - 1) as turn:
                slots(range(3, 3 + GROUP), turn)
            slots(range(ITEMS - 1, ITEMS + 3))

        def last_layer(item):
            return isinstance(item.layer, int) and item.layer == L - 1

        block = ctx.enter_context(nc.Block())

        @block.sync
        def _(sp):
            by_chunk = "(c p) d -> p c d"
            sp.dma_start(const[:, :], constants).then_inc(consts_in, 16)
            sp.dma_start(x_in[:, 0], x[0].rearrange(by_chunk, p=P)).then_inc(x_loaded[0], 16)
            sp.dma_start(kqv_raw[:, :, :], Wkqv.rearrange("l p n -> p l n")).then_inc(kqv_in, 16)
            for k in range(1, GROUP):
                sp.dma_start(x_in[:, k], x[k].rearrange(by_chunk, p=P)).then_inc(x_loaded[k], 16)
            sp.dma_start(wm1_raw[:, :, :], Wm1.rearrange("l p n -> p l n")).then_inc(wm1_in, 16)
            first = 0
            for source, halves in ((bm1, 2), (bm2, 1), (gn_g, 1), (gn_b, 1), (bf1, 2), (bf2, 1), (ln_g, 1), (ln_b, 1)):
                for h in range(halves):
                    sp.dma_start(rows[first:first + L, :], source[:, h * D:(h + 1) * D]).then_inc(rows_in, 16)
                    first += L
            sp.dma_start(gate_rows[:, :], Wg).then_inc(gate_in, 16)
            sp.dma_start(expert_rows[:, :, :], We.rearrange("e o d -> o e d")).then_inc(gate_in, 16)
            sp.wait_ge(ones_set, 1)
            for c in range(C):
                sp.dma_start(expert_b[E * c:E * c + E, c], be).then_inc(gate_in, 16)
            sp.dma_start(wm2_raw[:, :, :], Wm2.rearrange("l p n -> p l n")).then_inc(w_in, 16)
            sp.dma_start(wf1_raw[:, :, :], Wf1.rearrange("l p n -> p l n")).then_inc(w_in, 16)
            sp.dma_start(wf2_raw[:, :, :, :], Wf2.rearrange("l (h p) n -> p l h n", h=2)).then_inc(w_in, 16)
            sp.dma_start(ln_bc[:, 0], ln_g.partition_broadcast(P)).then_inc(bc_in, 16)
            sp.dma_start(ln_bc[:, 1], ln_b.partition_broadcast(P)).then_inc(bc_in, 16)
            for g in range(NG):
                for k in range(GROUP):
                    b = g * GROUP + k
                    sp.wait_ge(result_set, nth(g, k))
                    sp.dma_start(out[b].rearrange(by_chunk, p=P), result[:, k]).then_inc(stored[k], 16)
                    if g + 1 < NG:
                        sp.wait_ge(stored[k], 16 * (g + 1))
                        sp.dma_start(x_in[:, k], x[b + GROUP].rearrange(by_chunk, p=P)).then_inc(x_loaded[k], 16)
            for k in range(GROUP):
                sp.wait_ge(stored[k], 16 * NG)

        @block.tensor
        def _(pe):
            pe.wait_ge(consts_in, 16)
            pe.wait_ge(kqv_in, 16)
            for l in range(L):
                for j in range(3):
                    mm = pe.transpose(X1[:, j * D:(j + 1) * D], kqv_raw[:, l, j * D:(j + 1) * D], ident)
                mm.then_inc(turned, 1)
                if l == 0:
                    pe.wait_ge(wm1_in, 16)
                pe.wait_ge(turned_set, l + 1)
                if l:
                    pe.wait_ge(folded_set, l)
                pe.matmul(X2[:, 0:D], kqv_t[:, D:2 * D], kqv_t[:, 0:D], start=True, stop=True)
                pe.matmul(X3[:, 0:2 * D], kqv_t[:, 2 * D:], wm1_raw[:, l, :], start=True, stop=True).then_inc(folded, 1)
            pe.wait_ge(rows_in, 16 * 10)
            pe.transpose(Y1[:, 0:10 * L], rows[:, :], ident[0:10 * L, 0:10 * L]).then_inc(params_t, 1)
            pe.wait_ge(gate_in, 16 * (2 + C))
            pe.transpose(Y2[:, 0:E], gate_rows[:, :], ident[0:E, 0:E])
            for e in range(E):
                mm = pe.transpose((Z1, Z2)[e // HALF][:, e % HALF * D:(e % HALF + 1) * D], expert_rows[:, e, :], ident)
            mm.then_inc(gate_t, 1)
            pe.wait_ge(gate_set, 1)
            pe.wait_ge(params_set, 1)
            pe.wait_ge(folded_set, L)

            def take_in(k, g):
                pe.wait_ge(ha_set, pe.snap(ITEMS * g + k + 1))
                if k:
                    pe.wait_ge(logits_set, nth(g, k - 1))
                for c in range(C):
                    mm = pe.transpose(X1[:, c * P:(c + 1) * P], ha[:, k, c, 0:D], ident)
                mm.then_inc(h_turned, 1)
                pe.wait_ge(xnt_set, nth(g, k))
                for c in range(C):
                    mm = pe.matmul(X1[:, c * E:(c + 1) * E], xnt[:, k, c * P:(c + 1) * P], gate_w[:, :],
                                   start=True, stop=True)
                mm.then_inc(logits_done, 1)

            def route_biases(k, g):
                pe.wait_ge(route_set, g + 1)
                if k:
                    pe.wait_ge(bias_set, nth(g, k - 1))
                pe.transpose(X1[0:CE, 0:P], route[:, k * C:(k + 1) * C, :].rearrange("p c e -> p (c e)"),
                             ident).then_inc(route_turned, 1)
                pe.wait_ge(route_t_set, nth(g, k))
                pe.matmul(X1[:, :], route_t[:, k, :], expert_b[:, :, :].rearrange("p c d -> p (c d)"),
                          start=True, stop=True).then_inc(bias_done, 1)

            def experts(i, g):
                if i >= 2:
                    used = pe.snap(CHUNKS * g + i - 1)
                    pe.wait_ge(first_sum[HALF - 1], used)
                    pe.wait_ge(later_sum[HALF - 1], used)
                for h in range(2):
                    mm = pe.matmul(expert_banks[i % 2][h][:, :], xnt[:, i // C, i % C * P:(i % C + 1) * P],
                                   expert_w[:, h * HALF:(h + 1) * HALF, :].rearrange("p e d -> p (e d)"),
                                   start=True, stop=True)
                mm.then_inc(experts_done, 1)

            def slot(n, at, g):
                mine, mixing, feeding, finishing = at(n), at(n - 1), at(n - 2), at(n - 3)
                if mine:
                    k = mine.k
                    if k == 0:
                        pe.wait_ge(a_loaded, mine.layers)
                    pe.wait_ge(ht_set, mine.now)
                    pe.matmul(X1[:, :], a_w[:, :], ht[:, k, :], start=True, stop=True).then_inc(g_done, 1)
                if mixing:
                    k = mixing.k
                    pe.wait_ge(o_set, mixing.now)
                    for c in range(C):
                        mm = pe.transpose(Y2[:, c * P:(c + 1) * P], o_tok[:, c, :], ident)
                    mm.then_inc(ot_done, 1)
                if feeding:
                    k = feeding.k
                    if k == 0:
                        pe.wait_ge(feed_loaded, feeding.layers)
                    pe.wait_ge(gn_coef, feeding.now)
                    pe.matmul(Z1[:, 0:1], f1_w[:, 0:D], gn_c[:, :], start=True, stop=True)
                    pe.matmul(Z1[:, 1:2], f1_w[:, D:], gn_c[:, :], start=True, stop=True).then_inc(c_done, 1)
                if mine:
                    k = mine.k
                    pe.wait_ge(ha_set, mine.now)
                    for c in range(C - 1):
                        mm = pe.matmul(X2[:, c * AUG:c * AUG + D + 1], ha[:, k, c, 0:D], ha[:, k, c, 0:D + 1],
                                       start=True, stop=True)
                    mm.then_inc(gram_done, 1)
                if mixing:
                    k = mixing.k
                    if k == 0:
                        pe.wait_ge(mix_loaded, mixing.layers)
                    pe.wait_ge(ot_set, mixing.now)
                    pe.matmul(Y2[:, :], b_w[:, D:], ot[:, :], start=True, stop=True).then_inc(gate_done, 1)
                    if feeding:
                        pe.wait_ge(y_set, feeding.now)
                    pe.matmul(Y1[:, :], b_w[:, 0:D], ot[:, :], start=True, stop=True).then_inc(a_done, 1)
                if finishing and not last_layer(finishing):
                    k = finishing.k
                    pe.wait_ge(norm_set, finishing.now)
                    if feeding:
                        pe.wait_ge(c_set, feeding.now)
                    for c in range(C):
                        mm = pe.transpose(Z1[:, c * P:(c + 1) * P], norm[:, c, :], ident)
                    mm.then_inc(h_turned, 1)
                if mine:
                    k = mine.k
                    pe.wait_ge(gt_set, mine.now)
                    for c in range(C):
                        mm = pe.matmul(X3[:, c * P:(c + 1) * P], ht[:, k, c * P:(c + 1) * P], gt[:, c * P:(c + 1) * P],
                                       start=True, stop=True)
                    mm.then_inc(scores_done, 1)
                if feeding:
                    k = feeding.k
                    if finishing:
                        if last_layer(finishing):
                            pe.wait_ge(norm_set, finishing.now)
                        else:
                            pe.wait_ge(ht_set, finishing.next)
                    pe.wait_ge(c_set, feeding.now)
                    pe.wait_ge(y_set, feeding.now)
                    pe.matmul(Z1[:, :], f1_w[:, 0:D], y[:, k % 2, :], start=True, stop=True).then_inc(f1a_done, 1)
                    pe.matmul(Z2[:, :], f1_w[:, D:], y[:, k % 2, :], start=True, stop=True).then_inc(f1b_done, 1)
                if mixing:
                    k = mixing.k
                    pe.wait_ge(mixed_set, mixing.now)
                    pe.matmul(Y1[:, :], w2_w[:, :], mixed[:, :], start=True, stop=True).then_inc(mixed_done, 1)
                if feeding:
                    k = feeding.k
                    pe.wait_ge(gelu_a, feeding.now)
                    pe.matmul(Z1[:, :], f2_w[:, 0, :], gelu[:, 0, :], start=True, stop=False)
                    pe.wait_ge(gelu_b, feeding.now)
                    pe.matmul(Z1[:, :], f2_w[:, 1, :], gelu[:, 1, :], start=False, stop=True).then_inc(f2_done, 1)
                if mixing:
                    k = mixing.k
                    pe.wait_ge(gn_means, mixing.now)
                    pe.matmul(Y2[:, 0:1], mean_of[:, :], gn_m[:, :], start=True, stop=True).then_inc(gn_mean, 1)
                if mine:
                    k = mine.k
                    pe.wait_ge(past_set, mine.now)
                    pe.wait_ge(scores_set, mine.now)
                    for c in range(C):
                        dst = o_sums[:, c // 2, c % 2, 0:D + 1]
                        mm = pe.matmul(dst, scores[:, c * P:(c + 1) * P], ha[:, k, c, 0:D + 1],
                                       start=True, stop=(c == 0))
                        if c:
                            mm = pe.matmul(dst, gt[:, c * P:(c + 1) * P], past[:, c - 1, 0:D + 1],
                                           start=False, stop=True)
                    mm.then_inc(o_done, 1)
                if mixing:
                    k = mixing.k
                    pe.wait_ge(gn_parts, mixing.now)
                    pe.matmul(Y2[:, 0:1], mean_of[:, :], gn_p[:, :], start=True, stop=True).then_inc(gn_var, 1)
                if feeding:
                    k = feeding.k
                    pe.wait_ge(z_set, feeding.now)
                    for c in range(C):
                        mm = pe.transpose(Z2[:, c * P:(c + 1) * P], zt[:, c * P:(c + 1) * P], ident)
                    mm.then_inc(z_turned, 1)

            with pe.Fori(0, NG) as g:
                for k in range(GROUP):
                    take_in(k, g)
                for k in range(GROUP):
                    route_biases(k, g)
                for i in range(CHUNKS):
                    experts(i, g)
                pe.wait_ge(moe_set, pe.snap(CHUNKS * g + CHUNKS))
                run_slots(pe, g, slot)

        @block.scalar
        def _(act):
            for l in range(L):
                act.wait_ge(turned, l + 1)
                if l:
                    act.wait_ge(folded, l)
                act.copy(kqv_t[:, :], X1[:, 0:3 * D]).then_inc(turned_set, 1)
                act.wait_ge(folded, l + 1)
                act.mul(a_all[:, l, :], X2[:, 0:D], float(D) ** -0.5)
                act.copy(b_all[:, l, :], X3[:, 0:2 * D]).then_inc(folded_set, 1)
            act.wait_ge(params_t, 1)
            by_layer = Y1[:, 0:10 * L].rearrange("p (j l) -> p j l", l=L)
            act.copy(params[:, 0:HALF_B1G, :], by_layer[:, 0:2, :])
            act.mul(params[:, HALF_B1G, :], by_layer[:, B1G, :], 0.5)
            act.copy(params[:, B2:, :], by_layer[:, 2:, :]).then_inc(params_set, 1)
            act.wait_ge(gate_t, 1)
            act.copy(gate_w[:, :], Y2[:, 0:E])
            for h, half in enumerate((Z1, Z2)):
                last = act.copy(expert_w[:, h * HALF:(h + 1) * HALF, :].rearrange("p e d -> p (e d)"), half[:, :])
            last.then_inc(gate_set, 1)
            act.wait_ge(folded_set, L)
            act.wait_ge(params_set, 1)
            act.wait_ge(w_in, 16 * 3)
            act.wait_ge(bc_in, 32)

            def load_a(item):
                act.wait_ge(g_done, item.last)
                act.copy(a_w[:, :], a_all[:, item.layer, :]).then_inc(a_loaded, 1)

            def load_mix(item):
                if item.n:
                    act.wait_ge(gn_parts, item.last)
                act.copy(b_w[:, :], b_all[:, item.layer, :])
                act.mul(w2_w[:, :], wm2_raw[:, item.layer, :], 0.5)
                act.copy(mix_p[:, :], params[:, MIX, item.layer]).then_inc(mix_loaded, 1)

            def load_feed(item):
                if item.n:
                    act.wait_ge(z_set, item.last)
                act.copy(f1_w[:, :], wf1_raw[:, item.layer, :])
                act.copy(f2_w[:, :, :], wf2_raw[:, item.layer, :, :])
                act.copy(feed_p[:, :], params[:, FEED, item.layer]).then_inc(feed_loaded, 1)

            def slot(n, at, g):
                mine, mixing, feeding, finishing = at(n), at(n - 1), at(n - 2), at(n - 3)
                if mine:
                    act.wait_ge(g_done, mine.now)
                    act.copy(gt[:, :], X1[:, :]).then_inc(gt_set, 1)
                following = at(n + 1)
                if following and following.k == 0:
                    load_a(following)
                if mixing:
                    k = mixing.k
                    act.wait_ge(ot_done, mixing.now)
                    act.copy(ot[:, :], Y2[:, :]).then_inc(ot_set, 1)
                    if k == 0:
                        act.wait_ge(mix_loaded, mixing.layers)
                    act.wait_ge(gate_done, mixing.now)
                    act.activation(tanh_g[:, :], Y2[:, :], ACT.Tanh, bias=mix_p[:, 2:3], scale=0.5).then_inc(tanh_set, 1)
                    act.wait_ge(a_done, mixing.now)
                    act.activation(a_in[:, :], Y1[:, :], ACT.Identity, bias=mix_p[:, 0:1]).then_inc(a_set, 1)
                if finishing and not last_layer(finishing):
                    k = finishing.k
                    if k == 0:
                        act.wait_ge(finish_loaded, finishing.layers)
                    act.wait_ge(h_turned, finishing.next)
                    act.activation(ht[:, k, :], Z1[:, :], ACT.Identity, bias=finish_p[:, 1:2],
                                   scale=finish_p[:, 0:1]).then_inc(ht_set, 1)
                if feeding:
                    k = feeding.k
                    act.wait_ge(c_set, feeding.now)
                    act.wait_ge(f1a_done, feeding.now)
                    act.activation(gelu[:, 0, :], Z1[:, :], ACT.Gelu, bias=up_bias[:, 0:1]).then_inc(gelu_a, 1)
                    act.wait_ge(f1b_done, feeding.now)
                    act.activation(gelu[:, 1, :], Z2[:, :], ACT.Gelu, bias=up_bias[:, 1:2]).then_inc(gelu_b, 1)
                if mine and mine.k == 0:
                    load_mix(mine)
                if mixing and mixing.k == 0:
                    load_feed(mixing)
                if feeding and feeding.k == 0:
                    if feeding.n:
                        act.wait_ge(ha_set, feeding.count(feeding.n + GROUP))
                    act.copy(ln_w[:, :, :], ln_bc[:, :, feeding.layer, :])
                    act.copy(finish_p[:, :], params[:, FINISH, feeding.layer]).then_inc(finish_loaded, 1)

            with act.Fori(0, NG) as g:
                for k in range(GROUP):
                    act.wait_ge(h_turned, act.snap(ITEMS * g + k + 1))
                    act.copy(ht[:, k, :], X1[:, :]).then_inc(ht_set, 1)
                    act.copy(xnt[:, k, :], X1[:, :]).then_inc(xnt_set, 1)
                act.wait_ge(less_top, g + 1)
                act.activation(expo[:, :, :], expo[:, :, :], ACT.Exp).then_inc(expo_set, 1)
                for k in range(GROUP):
                    act.wait_ge(route_turned, nth(g, k))
                    act.copy(route_t[:, k, :], X1[0:CE, 0:P]).then_inc(route_t_set, 1)
                act.copy(a_w[:, :], a_all[:, 0, :]).then_inc(a_loaded, 1)
                run_slots(act, g, slot)

        @block.vector
        def _(dve):
            dve.memset(ha[:, :, :, D:], 1.0)
            dve.memset(mean_of[:, :], 1.0 / P)
            dve.memset(minus_half[:, :], -0.5)
            dve.memset(expert_b[:, :, :], 0.0).then_inc(ones_set, 1)

            def read_in(k, g):
                passed = dve.snap(16 * g + 16)
                dve.wait_ge(x_loaded[k], passed)
                for c in range(C):
                    last = dve.bn_stats(in_st[:, k, c, :], x_in[:, k, c, :])
                last.then_inc(in_stats[k], 16)
                dve.wait_ge(ones_set, 1)
                dve.wait_ge(in_stats[k], passed)
                for c in range(C):
                    last = dve.bn_aggr(in_mv[:, k, c, :], in_st[:, k, c, :])
                last.then_inc(in_aggr, 1)
                dve.wait_ge(in_aggr, nth(g, k))
                dve.tensor_scalar(in_v[:, k, :], in_mv[:, k, :, 1], EPS, None, ALU.add).then_inc(in_var, 1)

            def normalise_in(k, g):
                dve.wait_ge(in_rstd, nth(g, k))
                for c in range(C):
                    last = dve.tensor_scalar(ha[:, k, c, 0:D], x_in[:, k, c, :], in_mv[:, k, c, 0:1],
                                             in_r[:, k, c:c + 1], ALU.subtract, ALU.mult)
                last.then_inc(ha_set, 1)

            def route_all(g):
                one = (P, CHUNKS, E)
                sq = (P, CHUNKS, E, E)
                dve.wait_ge(logits_set, nth(g, GROUP - 1))
                dve.tensor_reduce(top[:, :], logits[:, :, :], AX.X, ALU.max).then_inc(top_set, 1)
                theirs = logits[:, :, :].unsqueeze(2).to_broadcast(sq)
                own = logits[:, :, :].unsqueeze(3).to_broadcast(sq)
                dve.tensor_tensor(ties[:, :, :, :], theirs, own, ALU.is_ge).then_inc(ties_set, 1)
                dve.wait_ge(top_set, g + 1)
                dve.tensor_tensor(expo[:, :, :], logits[:, :, :], top[:, :].unsqueeze(2).to_broadcast(one),
                                  ALU.subtract).then_inc(less_top, 1)
                dve.tensor_tensor(beats[:, :, :, :], theirs, own, ALU.is_gt).then_inc(beats_set, 1)
                dve.wait_ge(ties_set, 2 * g + 1)
                flat = (P, CHUNKS, E * E)
                dve.tensor_tensor(ties[:, :, :, :].rearrange("p c e f -> p c (e f)"),
                                  ties[:, :, :, :].rearrange("p c e f -> p c (e f)"),
                                  earlier.unsqueeze(1).to_broadcast(flat), ALU.mult).then_inc(ties_set, 1)
                dve.wait_ge(ties_set, 2 * g + 2)
                dve.wait_ge(beats_set, g + 1)
                dve.tensor_tensor(beats[:, :, :, :], beats[:, :, :, :], ties[:, :, :, :], ALU.max).then_inc(ranks_set, 1)
                dve.wait_ge(ranks_set, g + 1)
                dve.tensor_reduce(rank[:, :, :], beats[:, :, :, :], AX.X, ALU.add).then_inc(rank_set, 1)
                dve.wait_ge(rank_set, g + 1)
                dve.wait_ge(expo_set, g + 1)
                dve.scalar_tensor_tensor(share[:, :, :], rank[:, :, :], 2.0, expo[:, :, :], ALU.is_lt,
                                         ALU.mult).then_inc(share_set, 1)
                dve.wait_ge(share_set, g + 1)
                dve.tensor_reduce(total[:, :], share[:, :, :], AX.X, ALU.add).then_inc(total_set, 1)
                dve.wait_ge(total_set, g + 1)
                dve.reciprocal(total[:, :], total[:, :]).then_inc(inverse_set, 1)
                dve.wait_ge(inverse_set, g + 1)
                dve.tensor_tensor(route[:, :, :], share[:, :, :], total[:, :].unsqueeze(2).to_broadcast(one),
                                  ALU.mult).then_inc(route_set, 1)

            def add_experts(i, g):
                k, c = i // C, i % C
                now = dve.snap(CHUNKS * g + i + 1)
                dve.wait_ge(experts_done, now)
                if i == 0:
                    dve.wait_ge(route_set, g + 1)
                if c == 0:
                    dve.wait_ge(bias_set, nth(g, k))
                if i >= 2:
                    dve.wait_ge(moe_set, dve.snap(CHUNKS * g + i - 1))
                x_c, later = x_in[:, k, c, :], half_sum[:, i % 2, :]
                first_bank, later_bank = expert_banks[i % 2]
                for j in range(HALF):
                    if j:
                        dve.wait_ge(first_sum[j - 1], now)
                    cols = slice(j * D, (j + 1) * D)
                    dve.scalar_tensor_tensor(x_c, first_bank[:, cols], route[:, i, j:j + 1], x_c,
                                             ALU.mult, ALU.add).then_inc(first_sum[j], 1)
                    weight = route[:, i, HALF + j:HALF + j + 1]
                    if j:
                        dve.wait_ge(later_sum[j - 1], now)
                        dve.scalar_tensor_tensor(later, later_bank[:, cols], weight, later,
                                                 ALU.mult, ALU.add).then_inc(later_sum[j], 1)
                    else:
                        dve.tensor_scalar(later, later_bank[:, cols], weight, None, ALU.mult).then_inc(later_sum[j], 1)

            def join_experts(i, g):
                now = dve.snap(CHUNKS * g + i + 1)
                x_c = x_in[:, i // C, i % C, :]
                dve.wait_ge(first_sum[HALF - 1], now)
                dve.wait_ge(later_sum[HALF - 1], now)
                dve.tensor_tensor(x_c, x_c, half_sum[:, i % 2, :], ALU.add).then_inc(moe_set, 1)

            def slot(n, at, g):
                mine, mixing, feeding, finishing = at(n), at(n - 1), at(n - 2), at(n - 3)
                if mixing:
                    k = mixing.k
                    dve.wait_ge(o_done, mixing.now)
                    dve.tensor_tensor(den[:, 0], o_sums[:, :, :, D], norms, ALU.max).then_inc(den_one, 1)
                    dve.wait_ge(den_one, mixing.now)
                    dve.scalar_tensor_tensor(den[:, 1], o_sums[:, :, :, D], -1.0, den[:, 0],
                                             ALU.mult, ALU.max).then_inc(den_set, 1)
                    dve.wait_ge(den_set, mixing.now)
                    dve.reciprocal(den[:, 2], den[:, 1]).then_inc(inv_set, 1)
                    dve.wait_ge(inv_set, mixing.now)
                    dve.tensor_tensor(o_tok[:, :, :].rearrange("p (b c) d -> p b c d", b=2), o_sums[:, :, :, 0:D],
                                      den[:, 2].unsqueeze(3).to_broadcast((P, 2, 2, D)), ALU.mult).then_inc(o_set, 1)
                if finishing:
                    k = finishing.k
                    dve.wait_ge(z_turned, finishing.now)
                    for c in range(C):
                        last = dve.bn_stats(ln_stats[:, c, :], Z2[:, c * P:(c + 1) * P])
                    last.then_inc(ln_stats_set, 1)
                if feeding:
                    k = feeding.k
                    if k == 0:
                        dve.wait_ge(feed_loaded, feeding.layers)
                    dve.wait_ge(gn_rstd, feeding.now)
                    dve.tensor_tensor(gn_s[:, :], gn_r[:, :], feed_p[:, 0:1], ALU.mult).then_inc(gn_scale, 1)
                if finishing:
                    k = finishing.k
                    dve.wait_ge(ones_set, 1)
                    dve.wait_ge(ln_stats_set, finishing.now)
                    for c in range(C):
                        last = dve.bn_aggr(ln_mv[:, c, :], ln_stats[:, c, :])
                    last.then_inc(ln_aggr, 1)
                if feeding:
                    k = feeding.k
                    dve.wait_ge(gn_scale, feeding.now)
                    dve.scalar_tensor_tensor(gn_c[:, :], gn_b2[:, :], gn_s[:, 0:1], feed_p[:, 1:2],
                                             ALU.mult, ALU.add).then_inc(gn_coef, 1)
                if finishing:
                    k = finishing.k
                    dve.wait_ge(ln_aggr, finishing.now)
                    dve.tensor_scalar(ln_var[:, :], ln_mv[:, :, 1], EPS, None, ALU.add).then_inc(ln_veps, 1)
                if feeding:
                    k = feeding.k
                    dve.scalar_tensor_tensor(y[:, k % 2, :], Y1[:, :], gn_s[:, 0:1], ht[:, k, :],
                                             ALU.mult, ALU.add).then_inc(y_set, 1)
                    dve.wait_ge(gn_coef, feeding.now)
                    dve.tensor_tensor(z_bias[:, :], gn_c[:, :], feed_p[:, 4:5], ALU.add)
                    dve.wait_ge(c_done, feeding.now)
                    dve.tensor_tensor(up_bias[:, :], Z1[:, 0:2], feed_p[:, 2:4], ALU.add).then_inc(c_set, 1)
                if finishing:
                    k = finishing.k
                    dve.wait_ge(ln_rs, finishing.now)
                    if finishing.n:
                        dve.wait_ge(scaled_set, finishing.last)
                    for c in range(C):
                        last = dve.tensor_scalar(norm[:, c, :], Z2[:, c * P:(c + 1) * P], ln_mv[:, c, 0:1],
                                                 ln_rstd[:, c:c + 1], ALU.subtract, ALU.mult)
                    last.then_inc(norm_set, 1)
                if mine:
                    k = mine.k
                    dve.wait_ge(gram_done, mine.now)
                    dve.tensor_copy(past[:, 0, 0:D + 1], X2[:, 0:D + 1]).then_inc(past_one, 1)
                    dve.wait_ge(past_one, mine.now)
                    dve.tensor_tensor(past[:, 1, 0:D + 1], past[:, 0, 0:D + 1], X2[:, AUG:AUG + D + 1],
                                      ALU.add).then_inc(past_two, 1)
                    dve.wait_ge(past_two, mine.now)
                    dve.tensor_tensor(past[:, 2, 0:D + 1], past[:, 1, 0:D + 1], X2[:, 2 * AUG:2 * AUG + D + 1],
                                      ALU.add).then_inc(past_set, 1)
                if mixing:
                    k = mixing.k
                    if k == 0:
                        dve.wait_ge(mix_loaded, mixing.layers)
                    dve.wait_ge(a_set, mixing.now)
                    dve.scalar_tensor_tensor(gated[:, :], Y2[:, :], mix_p[:, 1:2], a_in[:, :],
                                             ALU.add, ALU.mult).then_inc(gated_set, 1)
                if mine:
                    k = mine.k
                    dve.wait_ge(scores_done, mine.now)
                    dve.tensor_tensor(scores[:, :].rearrange("p (c i) -> p c i", c=C),
                                      X3.rearrange("p (c i) -> p c i", c=C),
                                      causal.unsqueeze(1).to_broadcast((P, C, P)), ALU.mult).then_inc(scores_set, 1)
                if mixing:
                    k = mixing.k
                    dve.wait_ge(gated_set, mixing.now)
                    dve.scalar_tensor_tensor(mixed[:, :], tanh_g[:, :], 1.0, gated[:, :],
                                             ALU.add, ALU.mult).then_inc(mixed_set, 1)
                    dve.wait_ge(mixed_done, mixing.now)
                    dve.bn_stats(gn_st[:, :], Y1[:, :]).then_inc(gn_stats, 1)
                    dve.wait_ge(ones_set, 1)
                    dve.wait_ge(gn_stats, mixing.now)
                    dve.bn_aggr(gn_mv[:, :], gn_st[:, :]).then_inc(gn_aggr, 1)
                    dve.wait_ge(gn_aggr, mixing.now)
                    dve.tensor_tensor(gn_m[:, :], gn_mv[:, 0:1], mix_p[:, 3:4], ALU.add).then_inc(gn_means, 1)
                if feeding:
                    k = feeding.k
                    dve.wait_ge(f2_done, feeding.now)
                    dve.scalar_tensor_tensor(zt[:, :], Z1[:, :], z_bias[:, 0:1], y[:, k % 2, :],
                                             ALU.add, ALU.add).then_inc(z_set, 1)
                if mixing:
                    k = mixing.k
                    dve.wait_ge(gn_mean, mixing.now)
                    dve.wait_ge(gn_means, mixing.now)
                    dve.tensor_scalar(gn_d[:, :], Y2[:, 0:1], -1.0, gn_m[:, 0:1], ALU.mult, ALU.add).then_inc(gn_dev, 1)
                    dve.tensor_scalar(gn_b2[:, :], Y2[:, 0:1], -1.0, mix_p[:, 3:4], ALU.mult, ALU.add)
                    dve.wait_ge(gn_dev, mixing.now)
                    dve.scalar_tensor_tensor(gn_p[:, :], gn_d[:, :], gn_d[:, 0:1], gn_mv[:, 1:2],
                                             ALU.mult, ALU.add).then_inc(gn_parts, 1)
                    dve.wait_ge(gn_var, mixing.now)
                    dve.tensor_scalar(gn_v[:, :], Y2[:, 0:1], EPS, None, ALU.add).then_inc(gn_veps, 1)
                if finishing and last_layer(finishing):
                    k = finishing.k
                    dve.wait_ge(out_set, nth(g, k))
                    dve.tensor_tensor(result[:, k], result[:, k], x_in[:, k], ALU.add).then_inc(result_set, 1)

            with dve.Fori(0, NG) as g:
                for k in range(GROUP):
                    read_in(k, g)
                    if k:
                        normalise_in(k - 1, g)
                normalise_in(GROUP - 1, g)
                for k in range(GROUP):
                    dve.wait_ge(logits_done, nth(g, k))
                    dve.tensor_copy(logits[:, k * C:(k + 1) * C, :].rearrange("p c e -> p (c e)"),
                                    X1[:, 0:CE]).then_inc(logits_set, 1)
                route_all(g)
                for k in range(GROUP):
                    dve.wait_ge(bias_done, nth(g, k))
                    flat = x_in[:, k].rearrange("p c d -> p (c d)")
                    dve.tensor_tensor(flat, X1[:, :], flat, ALU.add).then_inc(bias_set, 1)
                for i in range(CHUNKS):
                    add_experts(i, g)
                    if i:
                        join_experts(i - 1, g)
                join_experts(CHUNKS - 1, g)
                run_slots(dve, g, slot)

        @block.gpsimd
        def _(pool):
            def slot(n, at, g):
                mixing, feeding, finishing = at(n - 1), at(n - 2), at(n - 3)
                if feeding:
                    k = feeding.k
                    pool.wait_ge(gn_veps, feeding.now)
                    pool.tensor_tensor(gn_r[:, :], gn_v[:, :], minus_half[:, 0:1], ALU.pow).then_inc(gn_rstd, 1)
                if finishing:
                    k = finishing.k
                    pool.wait_ge(ln_veps, finishing.now)
                    pool.tensor_tensor(ln_rstd[:, :], ln_var[:, :], minus_half[:, :], ALU.pow).then_inc(ln_rs, 1)
                    if k == 0:
                        pool.wait_ge(finish_loaded, finishing.layers)
                    pool.wait_ge(norm_set, finishing.now)
                    weights = [ln_w[:, j, :].unsqueeze(1).to_broadcast((P, C, D)) for j in range(2)]
                    pool.tensor_tensor(scaled[:, :, :], norm[:, :, :], weights[0], ALU.mult).then_inc(scaled_set, 1)
                    pool.wait_ge(scaled_set, finishing.now)
                    if last_layer(finishing):
                        pool.tensor_tensor(result[:, k], scaled[:, :, :], weights[1], ALU.add).then_inc(out_set, 1)
                    else:
                        pool.tensor_tensor(ha[:, k, :, 0:D], scaled[:, :, :], weights[1], ALU.add).then_inc(ha_set, 1)

            pool.wait_ge(ones_set, 1)
            with pool.Fori(0, NG) as g:
                for k in range(GROUP):
                    pool.wait_ge(in_var, nth(g, k))
                    pool.tensor_tensor(in_r[:, k, :], in_v[:, k, :], minus_half[:, :], ALU.pow).then_inc(in_rstd, 1)
                run_slots(pool, g, slot)


_INS = ['x', 'Wkqv', 'Wm1', 'bm1', 'Wm2', 'bm2', 'gn_g', 'gn_b', 'Wf1', 'bf1', 'Wf2', 'bf2', 'ln_g', 'ln_b']
_NAMES = [f"L0_attn_{name}" for name in _INS] + ['L0_ffn_Wg', 'L0_ffn_We', 'L0_ffn_be']


def _constants(tokens, experts):
    import numpy as np

    rank = np.arange(P)
    norm = 1 + np.sqrt(np.arange(tokens, dtype=np.float32))
    earlier = np.tril(np.ones((experts, experts)), -1).reshape(1, -1)
    return np.concatenate([np.eye(P), rank[:, None] <= rank[None, :], norm.reshape(-1, P).T,
                           np.repeat(earlier, P, 0)], 1).astype(np.float32)


def kernel(**inputs):
    import numpy as _np
    import concourse.bacc as _bacc
    from concourse import mybir as _mybir
    from concourse.bass_utils import run_bass_kernel_spmd as _run

    nc = _bacc.Bacc("TRN2", target_bir_lowering=False, num_devices=1)
    x, gate = inputs[_NAMES[0]], inputs['L0_ffn_Wg']
    arrays, args = {}, []
    for name in _NAMES:
        a = _np.ascontiguousarray(inputs[name])
        arrays[f"in_{name}_dram"] = a
        args.append(nc.dram_tensor(f"in_{name}_dram", a.shape, _mybir.dt.from_np(a.dtype), kind="ExternalInput").ap())
    consts = _constants(x.shape[1], gate.shape[0])
    arrays["constants_dram"] = consts
    args.append(nc.dram_tensor("constants_dram", consts.shape, F32, kind="ExternalInput").ap())
    args.append(nc.dram_tensor("out_0_dram", x.shape, F32, kind="ExternalOutput").ap())
    retention_moe(nc, *args)
    r = _run(nc, [arrays], core_ids=[0])
    return r.results[0]["out_0_dram"]
```

```python
from contextlib import ExitStack

import concourse.bass as bass
from concourse import mybir

F32 = mybir.dt.float32
F32R = mybir.dt.float32r
ALU = mybir.AluOpType
ACT = mybir.ActivationFunctionType
AX = mybir.AxisListType

P = 128
EPS = 1e-5
AUG = P + 2

B1A, B1G, HALF_B1G, B2, GN_G, GN_B, BF1A, BF1B, BF2, LN_G, LN_B = range(11)
MIX, FEED, FINISH = slice(B1A, GN_G), slice(GN_G, LN_G), slice(LN_G, LN_B + 1)


def retention_moe(nc, x, Wkqv, Wm1, bm1, Wm2, bm2, gn_g, gn_b, Wf1, bf1, Wf2, bf2, ln_g, ln_b,
                  Wg, We, be, constants, out):
    NB, S, D = x.shape
    L = Wkqv.shape[0]
    E = Wg.shape[0]
    C = S // P
    ITEMS = NB * L
    CHUNKS = NB * C
    CE = C * E
    HALF = E // 2
    BATCH = NB // 2
    RC = BATCH * C
    assert D == P and C == 4 and ITEMS == CHUNKS and RC * E == P

    ctx = ExitStack()
    with ctx:
        def sb(name, *shape, dtype=F32):
            return ctx.enter_context(nc.sbuf_tensor(name, list(shape), dtype))

        def bank(name):
            return ctx.enter_context(nc.psum_tensor(name, [P, 512], F32))

        def sem(name):
            return ctx.enter_context(nc.semaphore(name))

        const = sb("const", P, 2 * P + C + E * E)
        ident, causal = const[:, 0:P], const[:, P:2 * P]
        row_norm = const[:, 2 * P:2 * P + C]
        norms = row_norm.rearrange("p (b c) -> p b c", b=2)
        earlier = const[:, 2 * P + C:]
        mean_of = sb("mean_of", P, P)
        minus_half = sb("minus_half", P, C)
        kqv_raw = sb("kqv_raw", P, L, 3 * D)
        wm1_raw = sb("wm1_raw", P, L, 2 * D)
        wm2_raw = sb("wm2_raw", P, L, D)
        wf1_raw = sb("wf1_raw", P, L, 2 * D)
        wf2_raw = sb("wf2_raw", P, L, 2, D)
        kqv_t = sb("kqv_t", P, 2, 3 * D)
        a_all = sb("a_all", P, L, D)
        b_all = sb("b_all", P, L, 2 * D)
        rows = sb("rows", 10 * L, D)
        params = sb("params", P, 11, L)
        ln_bc = sb("ln_bc", P, 2, L, D)
        gate_rows = sb("gate_rows", E, D)
        gate_w = sb("gate_w", P, E)
        expert_rows = sb("expert_rows", P, E, D)
        expert_w = sb("expert_w", P, 2, E * D, dtype=F32R)
        expert_b = sb("expert_b", P, C, D)

        a_w = sb("a_w", P, D)
        b_w = sb("b_w", P, 2, 2 * D, dtype=F32R)
        w2_w = sb("w2_w", P, D)
        ln_w = sb("ln_w", P, 2, D)
        f1_w = sb("f1_w", P, 2, 2 * D, dtype=F32R)
        f2_w = sb("f2_w", P, 2, D)
        mix_p = sb("mix_p", P, 4)
        feed_p = sb("feed_p", P, 5)
        finish_p = sb("finish_p", P, 2)

        x_in = sb("x_in", P, NB, C, D)
        ht = sb("ht", P, NB, S)
        ha = sb("ha", P, NB, C, AUG)
        xnt = sb("xnt", P, CHUNKS, P)

        gt = sb("gt", P, S)
        past = sb("past", P, C - 1, AUG)
        scores = sb("scores", P, S)
        den = sb("den", P, 3, 2, 2)
        o_tok = sb("o_tok", P, C, D)
        ot = sb("ot", P, 2, S, dtype=F32R)
        tanh_g = sb("tanh_g", P, S)
        a_in = sb("a_in", P, S)
        gated = sb("gated", P, S)
        mixed = sb("mixed", P, S)
        gn_st = sb("gn_st", P, 6)
        gn_mv = sb("gn_mv", P, 2)
        gn_m = sb("gn_m", P, 1)
        gn_d = sb("gn_d", P, 1)
        gn_p = sb("gn_p", P, 1)
        gn_b2 = sb("gn_b2", P, 1)
        gn_v = sb("gn_v", P, 1)
        gn_r = sb("gn_r", P, 1)
        gn_s = sb("gn_s", P, 1)
        gn_c = sb("gn_c", P, 1)
        gn_out = sb("gn_out", P, S)
        y = sb("y", P, 2, S)
        y_parts = sb("y_parts", P, 2, S, dtype=F32R)
        gelu = sb("gelu", P, 2, S)
        zt = sb("zt", P, S)
        z_tok = sb("z_tok", P, C, D)
        ln_stats = sb("ln_stats", P, C, 6)
        ln_mv = sb("ln_mv", P, C, 2)
        ln_var = sb("ln_var", P, C)
        ln_rstd = sb("ln_rstd", P, C)
        ln_off = sb("ln_off", P, C)
        norm = sb("norm", P, C, D)
        scaled = sb("scaled", P, C, D)

        in_st = sb("in_st", P, NB, C, 6)
        in_mv = sb("in_mv", P, NB, C, 2)
        in_v = sb("in_v", P, NB, C)
        in_r = sb("in_r", P, NB, C)
        logits = sb("logits", P, RC, E)
        top = sb("top", P, RC)
        beats = sb("beats", P, RC, E, E)
        ties = sb("ties", P, RC, E, E)
        rank = sb("rank", P, RC, E)
        expo = sb("expo", P, RC, E)
        share = sb("share", P, RC, E)
        total = sb("total", P, RC)
        route = sb("route", P, CHUNKS, E)
        route_t = sb("route_t", P, P)

        chunk_t = sb("chunk_t", P, 2, 2, P, dtype=F32R)
        chunk_r = sb("chunk_r", P, 2, E)
        prod = sb("prod", P, E, D)
        sum_four = sb("sum_four", P, 4, D)
        sum_two = sb("sum_two", P, 2, D)
        sum_one = sb("sum_one", P, D)

        X1, X2, Y1, Y2, Z1, Z2 = (bank(b) for b in ("X1", "X2", "Y1", "Y2", "Z1", "Z2"))
        O = ctx.enter_context(nc.psum_tensor("O", [P, 2, 512], F32))
        X3, M1 = O[:, 0, :], O[:, 1, :]
        o_sums = O[:, :, 0:2 * AUG].rearrange("p b (c a) -> p b c a", c=2)

        def several(kind, names):
            return [kind(name) for name in names.split()]

        consts_in, kqv_in, wm1_in, w_in, rows_in, gate_in, experts_in, be_in, bc_in, ones_set = several(
            sem, "consts_in kqv_in wm1_in w_in rows_in gate_in experts_in be_in bc_in ones_set")
        turned, turned_set, folded, folded_set, params_t, params_set, gate_t, gate_set, expert_t, expert_rounded, expert_set = several(
            sem, "turned turned_set folded folded_set params_t params_set gate_t gate_set expert_t expert_rounded expert_set")
        x_loaded = [sem(f"x_loaded{k}") for k in range(NB)]
        in_stats, in_aggr, in_var, in_rstd, xnt_set, bias_done, bias_set, stored = several(
            sem, "in_stats in_aggr in_var in_rstd xnt_set bias_done bias_set stored")
        logits_done, logits_set, route_turned, route_t_set = several(
            sem, "logits_done logits_set route_turned route_t_set")
        top_set, less_top, expo_set, beats_set, ties_set, first_ties, ranks_set, rank_set, share_set, total_set, inverse_set, route_set = several(
            sem, "top_set less_top expo_set beats_set ties_set first_ties ranks_set rank_set share_set total_set inverse_set route_set")
        chunk_set, experts_a, experts_b, prod_a, prod_b, four_set, two_set, one_set, x_added = several(
            sem, "chunk_set experts_a experts_b prod_a prod_b four_set two_set one_set x_added")
        g_done, gram_done, scores_done, o_done = several(sem, "g_done gram_done scores_done o_done")
        gt_set, past_one, past_two, past_set, scores_set = several(sem, "gt_set past_one past_two past_set scores_set")
        den_one, den_set, inv_set, o_set = several(sem, "den_one den_set inv_set o_set")
        ot_done, ot_set, gate_done, a_done, tanh_set, a_set, gated_set, mixed_set, mixed_done = several(
            sem, "ot_done ot_set gate_done a_done tanh_set a_set gated_set mixed_set mixed_done")
        gn_stats, gn_aggr, gn_means, gn_mean, gn_dev, gn_parts, gn_var, gn_veps, gn_rstd, gn_scale, gn_coef = several(
            sem, "gn_stats gn_aggr gn_means gn_mean gn_dev gn_parts gn_var gn_veps gn_rstd gn_scale gn_coef")
        gn_done, y_set, f1a_done, f1b_done, gelu_a, gelu_b, f2_done, z_set = several(
            sem, "gn_done y_set f1a_done f1b_done gelu_a gelu_b f2_done z_set")
        z_turned, ln_stats_set, ln_aggr, ln_veps, ln_rs, norm_set, h_turned, ht_set, scaled_set, ha_set = several(
            sem, "z_turned ln_stats_set ln_aggr ln_veps ln_rs norm_set h_turned ht_set scaled_set ha_set")
        a_loaded, mix_loaded, feed_loaded, finish_loaded = several(
            sem, "a_loaded mix_loaded feed_loaded finish_loaded")
        result_set = sem("result_set")
        z_tok_set, ln_off_set, weights_set, b_rounded, b_set, f1_rounded, f1_set, ot_parts, y_rounded, y_rest, chunk_rounded = several(
            sem, "z_tok_set ln_off_set weights_set b_rounded b_set f1_rounded f1_set ot_parts y_rounded y_rest chunk_rounded")

        class Item:

            def __init__(self, n, layer, count):
                self.n, self.k, self.layer, self.layers, self.count = n, n % NB, layer, layer + 1, count

            last = property(lambda self: self.count(self.n))
            now = property(lambda self: self.count(self.n + 1))
            next = property(lambda self: self.count(self.n + 1 + NB))

        def slots(eng, numbers, slot, turn=None):
            counts = {}

            def count(items):
                if items not in counts:
                    counts[items] = items if turn is None else eng.snap(NB * turn + items)
                return counts[items]

            def at(j):
                if turn is None and not 0 <= j < ITEMS:
                    return None
                return Item(j, j // NB if turn is None else turn + j // NB, count)

            for n in numbers:
                slot(n, at)

        def full_slots(eng, slot):
            with eng.Fori(0, L - 1) as turn:
                slots(eng, range(3, 3 + NB), slot, turn)
            slots(eng, range(ITEMS - NB + 3, ITEMS + 3), slot)

        def last_layer(item):
            return isinstance(item.layer, int) and item.layer == L - 1

        block = ctx.enter_context(nc.Block())

        @block.sync
        def _(sp):
            by_chunk = "(c p) d -> p c d"
            sp.dma_start(const[:, :], constants).then_inc(consts_in, 16)
            sp.dma_start(x_in[:, 0], x[0].rearrange(by_chunk, p=P)).then_inc(x_loaded[0], 16)
            sp.dma_start(kqv_raw[:, :, :], Wkqv.rearrange("l p n -> p l n")).then_inc(kqv_in, 16)
            sp.dma_start(x_in[:, 1], x[1].rearrange(by_chunk, p=P)).then_inc(x_loaded[1], 16)
            sp.dma_start(wm1_raw[:, :, :], Wm1.rearrange("l p n -> p l n")).then_inc(wm1_in, 16)
            sp.dma_start(gate_rows[:, :], Wg).then_inc(gate_in, 16)
            for k in range(2, NB):
                sp.dma_start(x_in[:, k], x[k].rearrange(by_chunk, p=P)).then_inc(x_loaded[k], 16)
            first = 0
            for source, halves in ((bm1, 2), (bm2, 1), (gn_g, 1), (gn_b, 1), (bf1, 2), (bf2, 1), (ln_g, 1), (ln_b, 1)):
                for h in range(halves):
                    sp.dma_start(rows[first:first + L, :], source[:, h * D:(h + 1) * D]).then_inc(rows_in, 16)
                    first += L
            sp.dma_start(expert_rows[:, :, :], We.rearrange("e o d -> o e d")).then_inc(experts_in, 16)
            sp.dma_start(wm2_raw[:, :, :], Wm2.rearrange("l p n -> p l n")).then_inc(w_in, 16)
            sp.dma_start(wf1_raw[:, :, :], Wf1.rearrange("l p n -> p l n")).then_inc(w_in, 16)
            sp.dma_start(wf2_raw[:, :, :, :], Wf2.rearrange("l (h p) n -> p l h n", h=2)).then_inc(w_in, 16)
            sp.wait_ge(ones_set, 1)
            for j in range(P // E):
                sp.dma_start(expert_b[E * j:E * j + E, j % C], be).then_inc(be_in, 16)
            sp.dma_start(ln_bc[:, 0], ln_g.partition_broadcast(P)).then_inc(bc_in, 16)
            sp.dma_start(ln_bc[:, 1], ln_b.partition_broadcast(P)).then_inc(bc_in, 16)
            for k in range(NB):
                sp.wait_ge(result_set, k + 1)
                sp.dma_start(out[k].rearrange(by_chunk, p=P), x_in[:, k]).then_inc(stored, 16)
            sp.wait_ge(stored, 16 * NB)

        @block.tensor
        def _(pe):
            def product(dst, weights, moving):
                pe.matmul(dst, weights(0), moving(0), start=True, stop=False)
                pe.matmul(dst, weights(1), moving(0), start=False, stop=False)
                return pe.matmul(dst, weights(0), moving(1), start=False, stop=True)

            def turn_kqv(l):
                if l >= 2:
                    pe.wait_ge(turned_set, l - 1)
                for j in range(3):
                    mm = pe.transpose((X1, X2)[l % 2][:, j * D:(j + 1) * D], kqv_raw[:, l, j * D:(j + 1) * D], ident)
                mm.then_inc(turned, 1)

            def fold(l):
                pe.wait_ge(turned_set, l + 1)
                if l >= 2:
                    pe.wait_ge(folded_set, l - 1)
                bank, w = (X3, M1)[l % 2], kqv_t[:, l % 2]
                pe.matmul(bank[:, 0:D], w[:, D:2 * D], w[:, 0:D], start=True, stop=True)
                pe.matmul(bank[:, D:3 * D], w[:, 2 * D:], wm1_raw[:, l, :], start=True, stop=True).then_inc(folded, 1)

            def take_in(k):
                pe.wait_ge(ha_set, k + 1)
                if k >= 2:
                    pe.wait_ge(xnt_set, k - 1)
                for c in range(C):
                    mm = pe.transpose((Y1, Y2)[k % 2][:, c * P:(c + 1) * P], ha[:, k, c, 0:D], ident)
                mm.then_inc(h_turned, 1)

            def ask_gate(k):
                pe.wait_ge(xnt_set, k + 1)
                batch, j = divmod(k, BATCH)
                for c in range(C):
                    mm = pe.matmul((Z1, Z2)[batch][:, (j * C + c) * E:(j * C + c + 1) * E],
                                   xnt[:, k * C + c, :], gate_w[:, :], start=True, stop=True)
                if j == BATCH - 1:
                    mm.then_inc(logits_done, 1)

            def route_biases(batch, slot_before):
                pe.wait_ge(gt_set, slot_before + 1)
                pe.wait_ge(past_set, slot_before + 1)
                if batch:
                    pe.wait_ge(prod_a, slot_before - 1)
                    pe.wait_ge(prod_b, slot_before - 1)
                pe.wait_ge(route_set, batch + 1)
                pe.transpose(X1[:, 0:P], route[:, batch * RC:(batch + 1) * RC, :].rearrange("p c e -> p (c e)"),
                             ident).then_inc(route_turned, 1)
                pe.wait_ge(route_t_set, batch + 1)
                if not batch:
                    pe.wait_ge(be_in, 16 * (P // E))
                for j in range(BATCH):
                    if j >= 2:
                        pe.wait_ge(bias_set, batch * BATCH + j - 1)
                    of = slice(j * CE, (j + 1) * CE)
                    pe.matmul((X1, X2)[j % 2][:, :], route_t[of, :], expert_b[of, :, :].rearrange("p c d -> p (c d)"),
                              start=True, stop=True).then_inc(bias_done, 1)
                pe.wait_ge(bias_set, (batch + 1) * BATCH)

            pe.wait_ge(consts_in, 16)
            pe.wait_ge(kqv_in, 16)
            turn_kqv(0)
            turn_kqv(1)
            pe.wait_ge(wm1_in, 16)
            fold(0)
            pe.wait_ge(gate_in, 16)
            pe.transpose(Z2[:, 0:E], gate_rows[:, :], ident[0:E, 0:E]).then_inc(gate_t, 1)
            take_in(0)
            turn_kqv(2)
            fold(1)
            take_in(1)
            pe.wait_ge(gate_set, 1)
            ask_gate(0)
            turn_kqv(3)
            fold(2)
            take_in(2)
            ask_gate(1)
            fold(3)
            take_in(3)
            ask_gate(2)
            pe.wait_ge(rows_in, 16 * 10)
            pe.transpose(Z2[:, 0:10 * L], rows[:, :], ident[0:10 * L, 0:10 * L]).then_inc(params_t, 1)
            take_in(4)
            ask_gate(3)
            pe.wait_ge(params_set, 1)
            for k in range(5, NB):
                take_in(k)
                ask_gate(k - 1)
            pe.wait_ge(experts_in, 16)
            pe.wait_ge(folded_set, L)
            for e in range(E):
                mm = pe.transpose((X3, M1)[e // HALF][:, e % HALF * D:(e % HALF + 1) * D], expert_rows[:, e, :], ident)
            mm.then_inc(expert_t, 1)
            ask_gate(NB - 1)
            pe.wait_ge(expert_set, 1)

            def slot(n, at):
                mine, mixing, feeding, finishing = at(n), at(n - 1), at(n - 2), at(n - 3)
                if mine:
                    k = mine.k
                    if k == 0:
                        pe.wait_ge(a_loaded, mine.layers)
                    pe.wait_ge(ht_set, mine.now)
                    if finishing:
                        pe.wait_ge(prod_a, finishing.now)
                    pe.matmul(X1[:, :], a_w[:, :], ht[:, k, :], start=True, stop=True).then_inc(g_done, 1)
                if mixing:
                    pe.wait_ge(o_set, mixing.now)
                    for c in range(C):
                        mm = pe.transpose(Y2[:, c * P:(c + 1) * P], o_tok[:, c, :], ident)
                    mm.then_inc(ot_done, 1)
                if mine:
                    pe.wait_ge(ha_set, mine.now)
                    if finishing:
                        pe.wait_ge(prod_b, finishing.now)
                    for c in range(C - 1):
                        mm = pe.matmul(X2[:, c * AUG:c * AUG + D + 1], ha[:, k, c, 0:D], ha[:, k, c, 0:D + 1],
                                       start=True, stop=True)
                    mm.then_inc(gram_done, 1)
                    pe.wait_ge(gt_set, mine.now)
                    for c in range(C):
                        mm = pe.matmul(X3[:, c * P:(c + 1) * P], ht[:, k, c * P:(c + 1) * P], gt[:, c * P:(c + 1) * P],
                                       start=True, stop=True)
                    mm.then_inc(scores_done, 1)
                if mixing:
                    if mixing.k == 0:
                        pe.wait_ge(mix_loaded, mixing.layers)
                        pe.wait_ge(b_set, mixing.layers)
                    pe.wait_ge(ot_parts, mixing.now)
                    if feeding:
                        pe.wait_ge(gn_done, feeding.now)
                    product(Y1[:, :], lambda part: b_w[:, part, 0:D], lambda part: ot[:, part, :]).then_inc(a_done, 1)
                    product(Y2[:, :], lambda part: b_w[:, part, D:], lambda part: ot[:, part, :]).then_inc(gate_done, 1)
                if feeding:
                    pe.wait_ge(chunk_set, feeding.now)
                    if not mine:
                        pe.wait_ge(prod_a, finishing.now)
                    product(X1[:, :], lambda part: chunk_t[:, feeding.k % 2, part, :],
                            lambda part: expert_w[:, part, 0:HALF * D]).then_inc(experts_a, 1)
                if feeding:
                    if mine:
                        pe.wait_ge(past_set, mine.now)
                    else:
                        pe.wait_ge(prod_b, finishing.now)
                    product(X2[:, :], lambda part: chunk_t[:, feeding.k % 2, part, :],
                            lambda part: expert_w[:, part, HALF * D:]).then_inc(experts_b, 1)
                    if feeding.k == 0:
                        pe.wait_ge(feed_loaded, feeding.layers)
                        pe.wait_ge(f1_set, feeding.layers)
                    pe.wait_ge(y_rounded, feeding.now)
                    rounded, rest = y_parts[:, 0, :], y_parts[:, 1, :]
                    pe.matmul(Z2[:, :], f1_w[:, 0, D:], rounded, start=True, stop=False)
                    pe.matmul(Z2[:, :], f1_w[:, 1, D:], rounded, start=False, stop=False)
                    if finishing:
                        pe.wait_ge(z_tok_set, finishing.now)
                    pe.matmul(Z1[:, :], f1_w[:, 0, 0:D], rounded, start=True, stop=False)
                    pe.matmul(Z1[:, :], f1_w[:, 1, 0:D], rounded, start=False, stop=False)
                    pe.wait_ge(y_rest, feeding.now)
                    pe.matmul(Z2[:, :], f1_w[:, 0, D:], rest, start=False, stop=True).then_inc(f1b_done, 1)
                    pe.matmul(Z1[:, :], f1_w[:, 0, 0:D], rest, start=False, stop=True).then_inc(f1a_done, 1)
                if mixing:
                    pe.wait_ge(mixed_set, mixing.now)
                    pe.matmul(Y1[:, :], w2_w[:, :], mixed[:, :], start=True, stop=True).then_inc(mixed_done, 1)
                if feeding:
                    pe.wait_ge(gelu_b, feeding.now)
                    pe.matmul(Z2[:, :], f2_w[:, 1, :], gelu[:, 1, :], start=True, stop=False)
                    pe.wait_ge(gelu_a, feeding.now)
                    pe.matmul(Z2[:, :], f2_w[:, 0, :], gelu[:, 0, :], start=False, stop=True).then_inc(f2_done, 1)
                if finishing and not last_layer(finishing):
                    pe.wait_ge(norm_set, finishing.now)
                    for c in range(C):
                        mm = pe.transpose(Z1[:, c * P:(c + 1) * P], norm[:, c, :], ident)
                    mm.then_inc(h_turned, 1)
                if mixing:
                    pe.wait_ge(gn_means, mixing.now)
                    pe.matmul(Y2[:, 0:1], mean_of[:, :], gn_m[:, :], start=True, stop=True).then_inc(gn_mean, 1)
                if mine:
                    pe.wait_ge(past_set, mine.now)
                    pe.wait_ge(scores_set, mine.now)
                    for c in range(C):
                        dst = o_sums[:, c // 2, c % 2, 0:D + 1]
                        mm = pe.matmul(dst, scores[:, c * P:(c + 1) * P], ha[:, k, c, 0:D + 1],
                                       start=True, stop=(c == 0))
                        if c:
                            mm = pe.matmul(dst, gt[:, c * P:(c + 1) * P], past[:, c - 1, 0:D + 1],
                                           start=False, stop=True)
                    mm.then_inc(o_done, 1)
                if mixing:
                    pe.wait_ge(gn_parts, mixing.now)
                    pe.matmul(Y2[:, 0:1], mean_of[:, :], gn_p[:, :], start=True, stop=True).then_inc(gn_var, 1)
                if feeding:
                    if finishing and not last_layer(finishing):
                        pe.wait_ge(ht_set, finishing.next)
                    pe.wait_ge(z_set, feeding.now)
                    for c in range(C):
                        mm = pe.transpose(Z1[:, c * P:(c + 1) * P], zt[:, c * P:(c + 1) * P], ident)
                    mm.then_inc(z_turned, 1)

            slots(pe, [0, 1], slot)
            route_biases(0, 1)
            slots(pe, [2], slot)
            route_biases(1, 2)
            full_slots(pe, slot)

        @block.scalar
        def _(act):
            def set_kqv(l):
                act.wait_ge(turned, l + 1)
                if l >= 2:
                    act.wait_ge(folded, l - 1)
                act.copy(kqv_t[:, l % 2], (X1, X2)[l % 2][:, 0:3 * D]).then_inc(turned_set, 1)

            def set_folded(l):
                bank = (X3, M1)[l % 2]
                act.wait_ge(folded, l + 1)
                act.mul(a_all[:, l, :], bank[:, 0:D], float(D) ** -0.5)
                act.copy(b_all[:, l, :], bank[:, D:3 * D]).then_inc(folded_set, 1)

            def set_xnt(k):
                bank = (Y1, Y2)[k % 2]
                act.wait_ge(h_turned, k + 1)
                act.copy(ht[:, k, :], bank[:, :]).then_inc(ht_set, 1)
                act.copy(xnt[:, k * C:(k + 1) * C, :].rearrange("p c t -> p (c t)"), bank[:, :]).then_inc(xnt_set, 1)

            def exponents(batch):
                act.wait_ge(less_top, batch + 1)
                act.activation(expo[:, :, :], expo[:, :, :], ACT.Exp).then_inc(expo_set, 1)

            def turn_route(batch):
                act.wait_ge(route_turned, batch + 1)
                if batch:
                    act.wait_ge(bias_done, batch * BATCH)
                act.copy(route_t[:, :], X1[:, 0:P]).then_inc(route_t_set, 1)

            def load_a(item):
                act.wait_ge(g_done, item.last)
                act.copy(a_w[:, :], a_all[:, item.layer, :]).then_inc(a_loaded, 1)

            def load_mix(item):
                if item.n:
                    act.wait_ge(gn_parts, item.last)
                act.copy(b_w[:, 0, :], b_all[:, item.layer, :]).then_inc(b_rounded, 1)
                act.mul(w2_w[:, :], wm2_raw[:, item.layer, :], 0.5)
                act.copy(mix_p[:, :], params[:, MIX, item.layer]).then_inc(mix_loaded, 1)

            def load_feed(item):
                if item.n:
                    act.wait_ge(z_set, item.last)
                act.copy(f1_w[:, 0, :], wf1_raw[:, item.layer, :]).then_inc(f1_rounded, 1)
                act.copy(f2_w[:, :, :], wf2_raw[:, item.layer, :, :])
                act.copy(feed_p[:, :], params[:, FEED, item.layer]).then_inc(feed_loaded, 1)

            def slot(n, at):
                mine, mixing, feeding, finishing = at(n), at(n - 1), at(n - 2), at(n - 3)
                if finishing:
                    act.wait_ge(z_turned, finishing.now)
                    if finishing.n:
                        act.wait_ge(norm_set, finishing.last)
                    act.copy(z_tok[:, :, :].rearrange("p c d -> p (c d)"), Z1[:, :]).then_inc(z_tok_set, 1)
                if mine:
                    act.wait_ge(g_done, mine.now)
                    act.copy(gt[:, :], X1[:, :]).then_inc(gt_set, 1)
                following = at(n + 1)
                if following and following.k == 0:
                    load_a(following)
                if mixing:
                    act.wait_ge(ot_done, mixing.now)
                    act.copy(ot[:, 0, :], Y2[:, :]).then_inc(ot_set, 1)
                if feeding:
                    act.wait_ge(gn_coef, feeding.now)
                    act.activation(gn_out[:, :], Y1[:, :], ACT.Identity, bias=gn_c[:, 0:1],
                                   scale=gn_s[:, 0:1]).then_inc(gn_done, 1)
                if feeding:
                    act.wait_ge(y_set, feeding.now)
                    if finishing:
                        act.wait_ge(f1a_done, finishing.now)
                    act.copy(y_parts[:, 0, :], y[:, feeding.k % 2, :]).then_inc(y_rounded, 1)
                if mixing:
                    if mixing.k == 0:
                        act.wait_ge(mix_loaded, mixing.layers)
                    act.wait_ge(a_done, mixing.now)
                    act.activation(a_in[:, :], Y1[:, :], ACT.Identity, bias=mix_p[:, 0:1]).then_inc(a_set, 1)
                    act.wait_ge(gate_done, mixing.now)
                    act.activation(tanh_g[:, :], Y2[:, :], ACT.Tanh, bias=mix_p[:, 2:3], scale=0.5).then_inc(tanh_set, 1)
                if feeding:
                    act.wait_ge(f1b_done, feeding.now)
                    act.activation(gelu[:, 1, :], Z2[:, :], ACT.Gelu, bias=feed_p[:, 3:4]).then_inc(gelu_b, 1)
                    act.wait_ge(f1a_done, feeding.now)
                    act.activation(gelu[:, 0, :], Z1[:, :], ACT.Gelu, bias=feed_p[:, 2:3]).then_inc(gelu_a, 1)
                if finishing:
                    act.wait_ge(ln_off_set, finishing.now)
                    if finishing.n:
                        act.wait_ge(scaled_set, finishing.last)
                    for c in range(C):
                        last = act.activation(norm[:, c, :], z_tok[:, c, :], ACT.Identity, bias=ln_off[:, c:c + 1],
                                              scale=ln_rstd[:, c:c + 1])
                    last.then_inc(norm_set, 1)
                if mixing:
                    if n == 1:
                        act.wait_ge(route_set, 1)
                    if finishing:
                        act.wait_ge(experts_b, finishing.now)
                        act.wait_ge(prod_b, finishing.now)
                    act.copy(chunk_t[:, mixing.k % 2, 0, :], xnt[:, mixing.last, :]).then_inc(chunk_rounded, 1)
                    act.copy(chunk_r[:, mixing.k % 2, :], route[:, mixing.last, :]).then_inc(weights_set, 1)
                if finishing and not last_layer(finishing):
                    k = finishing.k
                    if k == 0:
                        act.wait_ge(finish_loaded, finishing.layers)
                    act.wait_ge(h_turned, finishing.next)
                    act.activation(ht[:, k, :], Z1[:, :], ACT.Identity, bias=finish_p[:, 1:2],
                                   scale=finish_p[:, 0:1]).then_inc(ht_set, 1)
                if mine and mine.k == 0:
                    load_mix(mine)
                if mixing and mixing.k == 0:
                    load_feed(mixing)
                if feeding and feeding.k == 0:
                    if feeding.n:
                        act.wait_ge(ha_set, feeding.count(feeding.n + NB))
                        act.wait_ge(ht_set, feeding.count(feeding.n + NB))
                    act.copy(ln_w[:, :, :], ln_bc[:, :, feeding.layer, :])
                    act.copy(finish_p[:, :], params[:, FINISH, feeding.layer]).then_inc(finish_loaded, 1)

            set_kqv(0)
            set_kqv(1)
            set_folded(0)
            act.wait_ge(gate_t, 1)
            act.copy(gate_w[:, :], Z2[:, 0:E]).then_inc(gate_set, 1)
            set_xnt(0)
            set_kqv(2)
            set_folded(1)
            set_xnt(1)
            set_kqv(3)
            set_folded(2)
            set_xnt(2)
            set_folded(3)
            set_xnt(3)
            act.wait_ge(folded_set, 1)
            act.copy(a_w[:, :], a_all[:, 0, :]).then_inc(a_loaded, 1)
            act.wait_ge(params_t, 1)
            by_layer = Z2[:, 0:10 * L].rearrange("p (j l) -> p j l", l=L)
            act.copy(params[:, 0:HALF_B1G, :], by_layer[:, 0:2, :])
            act.mul(params[:, HALF_B1G, :], by_layer[:, B1G, :], 0.5)
            act.copy(params[:, B2:, :], by_layer[:, 2:, :]).then_inc(params_set, 1)
            for k in range(4, NB):
                set_xnt(k)
            act.wait_ge(expert_t, 1)
            for h, half in enumerate((X3, M1)):
                last = act.copy(expert_w[:, 0, h * HALF * D:(h + 1) * HALF * D], half[:, :])
            last.then_inc(expert_rounded, 1)
            act.wait_ge(folded_set, L)
            act.wait_ge(params_set, 1)
            act.wait_ge(w_in, 16 * 3)
            act.wait_ge(bc_in, 32)
            act.wait_ge(xnt_set, NB)
            slots(act, [0], slot)
            exponents(0)
            slots(act, [1], slot)
            turn_route(0)
            exponents(1)
            slots(act, [2], slot)
            turn_route(1)
            full_slots(act, slot)

        @block.vector
        def _(dve):
            dve.memset(ha[:, :, :, D:], 1.0)
            dve.memset(mean_of[:, :], 1.0 / P)
            dve.memset(minus_half[:, :], -0.5)
            dve.memset(expert_b[:, :, :], 0.0).then_inc(ones_set, 1)

            def read_in(k):
                dve.wait_ge(x_loaded[k], 16)
                for c in range(C):
                    last = dve.bn_stats(in_st[:, k, c, :], x_in[:, k, c, :])
                last.then_inc(in_stats, 1)
                dve.wait_ge(in_stats, k + 1)
                for c in range(C):
                    last = dve.bn_aggr(in_mv[:, k, c, :], in_st[:, k, c, :])
                last.then_inc(in_aggr, 1)
                dve.wait_ge(in_aggr, k + 1)
                dve.tensor_scalar(in_v[:, k, :], in_mv[:, k, :, 1], EPS, None, ALU.add).then_inc(in_var, 1)

            def normalise_in(k):
                dve.wait_ge(in_rstd, k + 1)
                for c in range(C):
                    last = dve.tensor_scalar(ha[:, k, c, 0:D], x_in[:, k, c, :], in_mv[:, k, c, 0:1],
                                             in_r[:, k, c:c + 1], ALU.subtract, ALU.mult)
                last.then_inc(ha_set, 1)

            def route_batch(batch):
                one = (P, RC, E)
                sq = (P, RC, E, E)
                nth = batch + 1
                dve.wait_ge(logits_done, nth)
                if batch:
                    dve.wait_ge(route_set, batch)
                dve.tensor_copy(logits[:, :, :].rearrange("p c e -> p (c e)"),
                                (Z1, Z2)[batch][:, 0:RC * E]).then_inc(logits_set, 1)
                dve.wait_ge(logits_set, nth)
                dve.tensor_reduce(top[:, :], logits[:, :, :], AX.X, ALU.max).then_inc(top_set, 1)
                theirs = logits[:, :, :].unsqueeze(2).to_broadcast(sq)
                own = logits[:, :, :].unsqueeze(3).to_broadcast(sq)
                dve.tensor_tensor(ties[:, :, :, :], theirs, own, ALU.is_ge).then_inc(ties_set, 1)
                dve.wait_ge(top_set, nth)
                dve.tensor_tensor(expo[:, :, :], logits[:, :, :], top[:, :].unsqueeze(2).to_broadcast(one),
                                  ALU.subtract).then_inc(less_top, 1)
                dve.tensor_tensor(beats[:, :, :, :], theirs, own, ALU.is_gt).then_inc(beats_set, 1)
                dve.wait_ge(ties_set, nth)
                flat = (P, RC, E * E)
                dve.tensor_tensor(ties[:, :, :, :].rearrange("p c e f -> p c (e f)"),
                                  ties[:, :, :, :].rearrange("p c e f -> p c (e f)"),
                                  earlier.unsqueeze(1).to_broadcast(flat), ALU.mult).then_inc(first_ties, 1)
                dve.wait_ge(first_ties, nth)
                dve.wait_ge(beats_set, nth)
                dve.tensor_tensor(beats[:, :, :, :], beats[:, :, :, :], ties[:, :, :, :], ALU.max).then_inc(ranks_set, 1)
                dve.wait_ge(ranks_set, nth)
                dve.tensor_reduce(rank[:, :, :], beats[:, :, :, :], AX.X, ALU.add).then_inc(rank_set, 1)
                dve.wait_ge(rank_set, nth)
                dve.wait_ge(expo_set, nth)
                dve.scalar_tensor_tensor(share[:, :, :], rank[:, :, :], 2.0, expo[:, :, :], ALU.is_lt,
                                         ALU.mult).then_inc(share_set, 1)
                dve.wait_ge(share_set, nth)
                dve.tensor_reduce(total[:, :], share[:, :, :], AX.X, ALU.add).then_inc(total_set, 1)
                dve.wait_ge(total_set, nth)
                dve.reciprocal(total[:, :], total[:, :]).then_inc(inverse_set, 1)
                dve.wait_ge(inverse_set, nth)
                dve.tensor_tensor(route[:, batch * RC:(batch + 1) * RC, :], share[:, :, :],
                                  total[:, :].unsqueeze(2).to_broadcast(one), ALU.mult).then_inc(route_set, 1)

            def add_biases(batch):
                for j in range(BATCH):
                    k = batch * BATCH + j
                    dve.wait_ge(bias_done, k + 1)
                    flat = x_in[:, k].rearrange("p c d -> p (c d)")
                    dve.tensor_tensor(flat, (X1, X2)[j % 2][:, :], flat, ALU.add).then_inc(bias_set, 1)

            def weigh(which, bank, done, chunk):
                dve.wait_ge(done, chunk.now)
                experts = slice(which * HALF, (which + 1) * HALF)
                weights = chunk_r[:, chunk.k % 2, experts].unsqueeze(2).to_broadcast((P, HALF, D))
                dve.tensor_tensor(prod[:, experts, :], bank.rearrange("p (e d) -> p e d", e=HALF), weights,
                                  ALU.mult).then_inc((prod_a, prod_b)[which], 1)

            def slot(n, at):
                mine, mixing, feeding, finishing = at(n), at(n - 1), at(n - 2), at(n - 3)
                if mixing:
                    dve.wait_ge(o_done, mixing.now)
                    dve.tensor_tensor(den[:, 0], o_sums[:, :, :, D], norms, ALU.max).then_inc(den_one, 1)
                if feeding:
                    dve.wait_ge(gn_var, feeding.now)
                    dve.tensor_scalar(gn_v[:, :], Y2[:, 0:1], EPS, None, ALU.add).then_inc(gn_veps, 1)
                if mixing:
                    dve.wait_ge(den_one, mixing.now)
                    dve.scalar_tensor_tensor(den[:, 1], o_sums[:, :, :, D], -1.0, den[:, 0],
                                             ALU.mult, ALU.max).then_inc(den_set, 1)
                    dve.wait_ge(den_set, mixing.now)
                    dve.reciprocal(den[:, 2], den[:, 1]).then_inc(inv_set, 1)
                    dve.wait_ge(inv_set, mixing.now)
                    dve.tensor_tensor(o_tok[:, :, :].rearrange("p (b c) d -> p b c d", b=2), o_sums[:, :, :, 0:D],
                                      den[:, 2].unsqueeze(3).to_broadcast((P, 2, 2, D)), ALU.mult).then_inc(o_set, 1)
                if feeding:
                    if feeding.k == 0:
                        dve.wait_ge(feed_loaded, feeding.layers)
                    dve.wait_ge(gn_rstd, feeding.now)
                    dve.tensor_tensor(gn_s[:, :], gn_r[:, :], feed_p[:, 0:1], ALU.mult).then_inc(gn_scale, 1)
                    dve.wait_ge(gn_scale, feeding.now)
                    dve.scalar_tensor_tensor(gn_c[:, :], gn_b2[:, :], gn_s[:, 0:1], feed_p[:, 1:2],
                                             ALU.mult, ALU.add).then_inc(gn_coef, 1)
                if finishing:
                    dve.wait_ge(z_tok_set, finishing.now)
                    for c in range(C):
                        last = dve.bn_stats(ln_stats[:, c, :], z_tok[:, c, :])
                    last.then_inc(ln_stats_set, 1)
                if mixing:
                    dve.wait_ge(ot_set, mixing.now)
                    dve.tensor_tensor(ot[:, 1, :], Y2[:, :], ot[:, 0, :].bitcast(F32), ALU.subtract).then_inc(ot_parts, 1)
                    if mixing.k == 0:
                        dve.wait_ge(b_rounded, mixing.layers)
                        dve.tensor_tensor(b_w[:, 1, :], b_all[:, mixing.layer, :], b_w[:, 0, :].bitcast(F32),
                                          ALU.subtract).then_inc(b_set, 1)
                if feeding:
                    k = feeding.k
                    dve.wait_ge(gn_done, feeding.now)
                    dve.tensor_tensor(y[:, k % 2, :], gn_out[:, :], ht[:, k, :], ALU.add).then_inc(y_set, 1)
                if mine:
                    dve.wait_ge(gram_done, mine.now)
                    dve.tensor_copy(past[:, 0, 0:D + 1], X2[:, 0:D + 1]).then_inc(past_one, 1)
                    dve.wait_ge(past_one, mine.now)
                    dve.tensor_tensor(past[:, 1, 0:D + 1], past[:, 0, 0:D + 1], X2[:, AUG:AUG + D + 1],
                                      ALU.add).then_inc(past_two, 1)
                    dve.wait_ge(past_two, mine.now)
                    dve.tensor_tensor(past[:, 2, 0:D + 1], past[:, 1, 0:D + 1], X2[:, 2 * AUG:2 * AUG + D + 1],
                                      ALU.add).then_inc(past_set, 1)
                if finishing:
                    dve.wait_ge(ones_set, 1)
                    dve.wait_ge(ln_stats_set, finishing.now)
                    for c in range(C):
                        last = dve.bn_aggr(ln_mv[:, c, :], ln_stats[:, c, :])
                    last.then_inc(ln_aggr, 1)
                if feeding and feeding.k == 0:
                    dve.wait_ge(f1_rounded, feeding.layers)
                    dve.tensor_tensor(f1_w[:, 1, :], wf1_raw[:, feeding.layer, :], f1_w[:, 0, :].bitcast(F32),
                                      ALU.subtract).then_inc(f1_set, 1)
                if mine:
                    dve.wait_ge(scores_done, mine.now)
                    dve.tensor_tensor(scores[:, :].rearrange("p (c i) -> p c i", c=C),
                                      X3.rearrange("p (c i) -> p c i", c=C),
                                      causal.unsqueeze(1).to_broadcast((P, C, P)), ALU.mult).then_inc(scores_set, 1)
                if mixing:
                    if mixing.k == 0:
                        dve.wait_ge(mix_loaded, mixing.layers)
                    dve.wait_ge(a_set, mixing.now)
                    dve.wait_ge(tanh_set, mixing.now)
                    dve.scalar_tensor_tensor(gated[:, :], Y2[:, :], mix_p[:, 1:2], a_in[:, :],
                                             ALU.add, ALU.mult).then_inc(gated_set, 1)
                if finishing:
                    dve.wait_ge(ln_aggr, finishing.now)
                    dve.tensor_scalar(ln_var[:, :], ln_mv[:, :, 1], EPS, None, ALU.add).then_inc(ln_veps, 1)
                if mixing:
                    dve.wait_ge(gated_set, mixing.now)
                    dve.scalar_tensor_tensor(mixed[:, :], tanh_g[:, :], 1.0, gated[:, :],
                                             ALU.add, ALU.mult).then_inc(mixed_set, 1)
                if finishing:
                    dve.wait_ge(ln_rs, finishing.now)
                    dve.scalar_tensor_tensor(ln_off[:, :], ln_mv[:, :, 0], -1.0, ln_rstd[:, :],
                                             ALU.mult, ALU.mult).then_inc(ln_off_set, 1)
                if mixing:
                    dve.wait_ge(mixed_done, mixing.now)
                    dve.bn_stats(gn_st[:, :], Y1[:, :]).then_inc(gn_stats, 1)
                if feeding:
                    if finishing:
                        dve.wait_ge(four_set, finishing.now)
                    dve.wait_ge(weights_set, feeding.now)
                    weigh(0, X1, experts_a, feeding)
                if mixing:
                    dve.wait_ge(ones_set, 1)
                    dve.wait_ge(gn_stats, mixing.now)
                    dve.bn_aggr(gn_mv[:, :], gn_st[:, :]).then_inc(gn_aggr, 1)
                    dve.wait_ge(gn_aggr, mixing.now)
                    dve.tensor_tensor(gn_m[:, :], gn_mv[:, 0:1], mix_p[:, 3:4], ALU.add).then_inc(gn_means, 1)
                if feeding:
                    weigh(1, X2, experts_b, feeding)
                if finishing:
                    x_chunk = x_in[:, :, :, :].rearrange("p k c d -> p (k c) d")[:, finishing.last, :]
                    dve.wait_ge(one_set, finishing.now)
                    dve.tensor_tensor(x_chunk, x_chunk, sum_one[:, :], ALU.add).then_inc(x_added, 1)
                if feeding:
                    dve.wait_ge(f2_done, feeding.now)
                    dve.scalar_tensor_tensor(zt[:, :], Z2[:, :], feed_p[:, 4:5], y[:, feeding.k % 2, :],
                                             ALU.add, ALU.add).then_inc(z_set, 1)
                if mixing:
                    dve.wait_ge(gn_mean, mixing.now)
                    dve.wait_ge(gn_means, mixing.now)
                    dve.tensor_scalar(gn_d[:, :], Y2[:, 0:1], -1.0, gn_m[:, 0:1], ALU.mult, ALU.add).then_inc(gn_dev, 1)
                    dve.tensor_scalar(gn_b2[:, :], Y2[:, 0:1], -1.0, mix_p[:, 3:4], ALU.mult, ALU.add)
                    dve.wait_ge(gn_dev, mixing.now)
                    dve.scalar_tensor_tensor(gn_p[:, :], gn_d[:, :], gn_d[:, 0:1], gn_mv[:, 1:2],
                                             ALU.mult, ALU.add).then_inc(gn_parts, 1)
                    dve.wait_ge(chunk_rounded, mixing.now)
                    parts = chunk_t[:, mixing.k % 2]
                    dve.tensor_tensor(parts[:, 1, :], xnt[:, mixing.last, :], parts[:, 0, :].bitcast(F32),
                                      ALU.subtract).then_inc(chunk_set, 1)
                if finishing and last_layer(finishing):
                    k = finishing.k
                    dve.wait_ge(ha_set, finishing.next)
                    dve.wait_ge(x_added, finishing.now)
                    dve.tensor_tensor(x_in[:, k], ha[:, k, :, 0:D], x_in[:, k], ALU.add).then_inc(result_set, 1)

            for k in range(NB):
                read_in(k)
                if k:
                    normalise_in(k - 1)
            normalise_in(NB - 1)
            dve.wait_ge(expert_rounded, 1)
            for h, half in enumerate((X3, M1)):
                cols = slice(h * HALF * D, (h + 1) * HALF * D)
                last = dve.tensor_tensor(expert_w[:, 1, cols], half[:, :], expert_w[:, 0, cols].bitcast(F32), ALU.subtract)
            last.then_inc(expert_set, 1)
            slots(dve, [0], slot)
            route_batch(0)
            slots(dve, [1], slot)
            add_biases(0)
            route_batch(1)
            slots(dve, [2], slot)
            add_biases(1)
            dve.wait_ge(bias_set, NB)
            full_slots(dve, slot)

        @block.gpsimd
        def _(pool):
            def slot(n, at):
                feeding, finishing = at(n - 2), at(n - 3)
                if feeding:
                    pool.wait_ge(gn_veps, feeding.now)
                    pool.tensor_tensor(gn_r[:, :], gn_v[:, :], minus_half[:, 0:1], ALU.pow).then_inc(gn_rstd, 1)
                if finishing:
                    pool.wait_ge(prod_a, finishing.now)
                    pool.wait_ge(prod_b, finishing.now)
                    pool.tensor_tensor(sum_four[:, :, :], prod[:, 0:4, :], prod[:, 4:8, :], ALU.add).then_inc(four_set, 1)
                    pool.wait_ge(four_set, finishing.now)
                    pool.tensor_tensor(sum_two[:, :, :], sum_four[:, 0:2, :], sum_four[:, 2:4, :], ALU.add).then_inc(two_set, 1)
                if finishing:
                    pool.wait_ge(two_set, finishing.now)
                    if finishing.n:
                        pool.wait_ge(x_added, finishing.last)
                    pool.tensor_tensor(sum_one[:, :], sum_two[:, 0, :], sum_two[:, 1, :], ALU.add).then_inc(one_set, 1)
                if feeding:
                    pool.wait_ge(y_rounded, feeding.now)
                    pool.tensor_tensor(y_parts[:, 1, :], y[:, feeding.k % 2, :], y_parts[:, 0, :].bitcast(F32),
                                       ALU.subtract).then_inc(y_rest, 1)
                if finishing:
                    k = finishing.k
                    pool.wait_ge(ln_veps, finishing.now)
                    pool.tensor_tensor(ln_rstd[:, :], ln_var[:, :], minus_half[:, :], ALU.pow).then_inc(ln_rs, 1)
                    if k == 0:
                        pool.wait_ge(finish_loaded, finishing.layers)
                    pool.wait_ge(norm_set, finishing.now)
                    weights = [ln_w[:, j, :].unsqueeze(1).to_broadcast((P, C, D)) for j in range(2)]
                    pool.tensor_tensor(scaled[:, :, :], norm[:, :, :], weights[0], ALU.mult).then_inc(scaled_set, 1)
                    pool.wait_ge(scaled_set, finishing.now)
                    pool.tensor_tensor(ha[:, k, :, 0:D], scaled[:, :, :], weights[1], ALU.add).then_inc(ha_set, 1)

            pool.wait_ge(ones_set, 1)
            for k in range(NB):
                pool.wait_ge(in_var, k + 1)
                pool.tensor_tensor(in_r[:, k, :], in_v[:, k, :], minus_half[:, :], ALU.pow).then_inc(in_rstd, 1)
            slots(pool, range(3), slot)
            full_slots(pool, slot)


_INS = ['x', 'Wkqv', 'Wm1', 'bm1', 'Wm2', 'bm2', 'gn_g', 'gn_b', 'Wf1', 'bf1', 'Wf2', 'bf2', 'ln_g', 'ln_b']
_NAMES = [f"L0_attn_{name}" for name in _INS] + ['L0_ffn_Wg', 'L0_ffn_We', 'L0_ffn_be']


def _constants(tokens, experts):
    import numpy as np

    rank = np.arange(P)
    norm = 1 + np.sqrt(np.arange(tokens, dtype=np.float32))
    earlier = np.tril(np.ones((experts, experts)), -1).reshape(1, -1)
    return np.concatenate([np.eye(P), rank[:, None] <= rank[None, :], norm.reshape(-1, P).T,
                           np.repeat(earlier, P, 0)], 1).astype(np.float32)


def kernel(**inputs):
    import numpy as _np
    import concourse.bacc as _bacc
    from concourse import mybir as _mybir
    from concourse.bass_utils import run_bass_kernel_spmd as _run

    nc = _bacc.Bacc("TRN2", target_bir_lowering=False, num_devices=1)
    x, gate = inputs[_NAMES[0]], inputs['L0_ffn_Wg']
    arrays, args = {}, []
    for name in _NAMES:
        a = _np.ascontiguousarray(inputs[name])
        arrays[f"in_{name}_dram"] = a
        args.append(nc.dram_tensor(f"in_{name}_dram", a.shape, _mybir.dt.from_np(a.dtype), kind="ExternalInput").ap())
    consts = _constants(x.shape[1], gate.shape[0])
    arrays["constants_dram"] = consts
    args.append(nc.dram_tensor("constants_dram", consts.shape, F32, kind="ExternalInput").ap())
    args.append(nc.dram_tensor("out_0_dram", x.shape, F32, kind="ExternalOutput").ap())
    retention_moe(nc, *args)
    r = _run(nc, [arrays], core_ids=[0])
    return r.results[0]["out_0_dram"]
```

```python
from contextlib import ExitStack

import concourse.bass as bass
from concourse import mybir

F32 = mybir.dt.float32
F32R = mybir.dt.float32r
ALU = mybir.AluOpType
ACT = mybir.ActivationFunctionType
AX = mybir.AxisListType

P = 128
EPS = 1e-5
AUG = P + 2

B1A, B1G, HALF_B1G, B2, GN_G, GN_B, BF1A, BF1B, BF2, LN_G, LN_B = range(11)
MIX, FEED, FINISH = slice(B1A, GN_G), slice(GN_G, LN_G), slice(LN_G, LN_B + 1)


def retention_moe(nc, x, Wkqv, Wm1, bm1, Wm2, bm2, gn_g, gn_b, Wf1, bf1, Wf2, bf2, ln_g, ln_b,
                  Wg, We, be, constants, out):
    NB, S, D = x.shape
    L = Wkqv.shape[0]
    E = Wg.shape[0]
    C = S // P
    ITEMS = NB * L
    CHUNKS = NB * C
    CE = C * E
    HALF = E // 2
    BATCH = NB // 2
    RC = BATCH * C
    assert D == P and C == 4 and ITEMS == CHUNKS and RC * E == P

    ctx = ExitStack()
    with ctx:
        def sb(name, *shape, dtype=F32):
            return ctx.enter_context(nc.sbuf_tensor(name, list(shape), dtype))

        def bank(name):
            return ctx.enter_context(nc.psum_tensor(name, [P, 512], F32))

        def sem(name):
            return ctx.enter_context(nc.semaphore(name))

        const = sb("const", P, 2 * P + C + E)
        ident, causal = const[:, 0:P], const[:, P:2 * P]
        row_norm = const[:, 2 * P:2 * P + C]
        norms = row_norm.rearrange("p (b c) -> p b c", b=2)
        preference = const[:, 2 * P + C:]
        mean_of = sb("mean_of", P, P)
        minus_half = sb("minus_half", P, C)
        kqv_raw = sb("kqv_raw", P, L, 3 * D)
        wm1_raw = sb("wm1_raw", P, L, 2 * D)
        wm2_raw = sb("wm2_raw", P, L, D)
        wf1_raw = sb("wf1_raw", P, L, 2 * D)
        wf2_raw = sb("wf2_raw", P, L, 2, D)
        kqv_t = sb("kqv_t", P, 2, 3 * D)
        a_all = sb("a_all", P, L, D)
        b_all = sb("b_all", P, L, 2 * D)
        rows = sb("rows", 10 * L, D)
        params = sb("params", P, 11, L)
        ln_bc = sb("ln_bc", P, 2, L, D)
        gate_rows = sb("gate_rows", E, D)
        gate_w = sb("gate_w", P, E)
        expert_rows = sb("expert_rows", P, E, D)
        expert_w = sb("expert_w", P, 2, E * D, dtype=F32R)
        expert_b = sb("expert_b", P, C, D)

        a_w = sb("a_w", P, 2, D, dtype=F32R)
        b_w = sb("b_w", P, 2, 2 * D, dtype=F32R)
        w2_w = sb("w2_w", P, D)
        ln_w = sb("ln_w", P, 2, D)
        f1_w = sb("f1_w", P, 2, 2 * D, dtype=F32R)
        f2_w = sb("f2_w", P, 2, D)
        mix_p = sb("mix_p", P, 4)
        feed_p = sb("feed_p", P, 5)
        finish_p = sb("finish_p", P, 2)

        x_in = sb("x_in", P, NB, C, D)
        ht = sb("ht", P, NB, S)
        ha = sb("ha", P, NB, C, AUG)
        xnt = sb("xnt", P, CHUNKS, P)

        h_parts = sb("h_parts", P, 2, S, dtype=F32R)
        gt = sb("gt", P, S)
        past = sb("past", P, C - 1, AUG)
        scores = sb("scores", P, S)
        den = sb("den", P, 3, 2, 2)
        o_tok = sb("o_tok", P, C, D)
        ot = sb("ot", P, 2, S, dtype=F32R)
        tanh_g = sb("tanh_g", P, S)
        a_in = sb("a_in", P, S)
        gated = sb("gated", P, S)
        mixed = sb("mixed", P, S)
        gn_st = sb("gn_st", P, 6)
        gn_mv = sb("gn_mv", P, 2)
        gn_m = sb("gn_m", P, 1)
        gn_d = sb("gn_d", P, 1)
        gn_p = sb("gn_p", P, 1)
        gn_b2 = sb("gn_b2", P, 1)
        gn_v = sb("gn_v", P, 1)
        gn_r = sb("gn_r", P, 1)
        gn_s = sb("gn_s", P, 1)
        gn_c = sb("gn_c", P, 1)
        gn_out = sb("gn_out", P, S)
        y = sb("y", P, 2, S)
        y_parts = sb("y_parts", P, 2, S, dtype=F32R)
        gelu = sb("gelu", P, 2, S)
        zt = sb("zt", P, S)
        z_tok = sb("z_tok", P, C, D)
        ln_stats = sb("ln_stats", P, C, 6)
        ln_mv = sb("ln_mv", P, C, 2)
        ln_var = sb("ln_var", P, C)
        ln_rstd = sb("ln_rstd", P, C)
        ln_off = sb("ln_off", P, C)
        norm = sb("norm", P, C, D)
        scaled = sb("scaled", P, C, D)

        in_st = sb("in_st", P, NB, C, 6)
        in_mv = sb("in_mv", P, NB, C, 2)
        in_v = sb("in_v", P, NB, C)
        in_r = sb("in_r", P, NB, C)
        logits = sb("logits", P, CHUNKS, E)
        second = sb("second", P, CHUNKS, E)
        best = sb("best", P, 2, CHUNKS)
        ties = sb("ties", P, 2, CHUNKS, E)
        favour = sb("favour", P, 2, CHUNKS, E)
        choice = sb("choice", P, 2, CHUNKS)
        chosen = sb("chosen", P, 2, CHUNKS, E)
        both = sb("both", P, CHUNKS, E)
        expo = sb("expo", P, CHUNKS, E)
        share = sb("share", P, CHUNKS, E)
        total = sb("total", P, 2, CHUNKS)
        route = sb("route", P, CHUNKS, E)
        route_t = sb("route_t", P, 2, P)

        chunk_t = sb("chunk_t", P, 2, 2, P, dtype=F32R)
        chunk_r = sb("chunk_r", P, 2, E)
        prod = sb("prod", P, E, D)
        sum_four = sb("sum_four", P, 4, D)
        sum_two = sb("sum_two", P, 2, D)
        sum_one = sb("sum_one", P, D)

        X1, X2, Y1, Y2, Z1, Z2 = (bank(b) for b in ("X1", "X2", "Y1", "Y2", "Z1", "Z2"))
        O = ctx.enter_context(nc.psum_tensor("O", [P, 2, 512], F32))
        X3, M1 = O[:, 0, :], O[:, 1, :]
        o_sums = O[:, :, 0:2 * AUG].rearrange("p b (c a) -> p b c a", c=2)

        def several(kind, names):
            return [kind(name) for name in names.split()]

        consts_in, kqv_in, wm1_in, wm2_in, wf_in, rows_in, gate_in, experts_in, be_in, bc_in, ones_set = several(
            sem, "consts_in kqv_in wm1_in wm2_in wf_in rows_in gate_in experts_in be_in bc_in ones_set")
        (turned, turned_set, folded, folded_set, params_t,
         params_set, gate_t, gate_set, expert_t, expert_rounded, expert_set) = several(
            sem, "turned turned_set folded folded_set params_t "
                 "params_set gate_t gate_set expert_t expert_rounded expert_set")
        x_loaded = [sem(f"x_loaded{k}") for k in range(NB)]
        in_stats, in_aggr, in_var, in_rstd, xnt_set, bias_done, bias_set, stored = several(
            sem, "in_stats in_aggr in_var in_rstd xnt_set bias_done bias_set stored")
        logits_done, logits_set, route_turned, route_t_set, less_top, expo_set, route_set = several(
            sem, "logits_done logits_set route_turned route_t_set less_top expo_set route_set")
        (best_set, ties_set, favour_set, choice_set, chosen_set,
         second_set, both_set, share_set, total_set, inverse_set) = several(
            sem, "best_set ties_set favour_set choice_set chosen_set "
                 "second_set both_set share_set total_set inverse_set")
        chunk_set, experts_a, experts_b, prod_a, prod_b, four_set, two_set, one_set, x_added = several(
            sem, "chunk_set experts_a experts_b prod_a prod_b four_set two_set one_set x_added")
        g_done, gram_done, scores_done, o_done = several(sem, "g_done gram_done scores_done o_done")
        gt_set, past_one, past_two, past_set, scores_set = several(sem, "gt_set past_one past_two past_set scores_set")
        den_one, den_set, inv_set, o_half, o_set = several(sem, "den_one den_set inv_set o_half o_set")
        ot_done, ot_set, gate_done, a_done, tanh_set, a_set, gated_set, mixed_set, mixed_done = several(
            sem, "ot_done ot_set gate_done a_done tanh_set a_set gated_set mixed_set mixed_done")
        gn_stats, gn_aggr, gn_means, gn_mean, gn_dev, gn_parts, gn_var, gn_veps, gn_rstd, gn_scale, gn_coef = several(
            sem, "gn_stats gn_aggr gn_means gn_mean gn_dev gn_parts gn_var gn_veps gn_rstd gn_scale gn_coef")
        gn_done, y_set, f1a_done, f1b_done, gelu_a, gelu_b, f2_done, z_set = several(
            sem, "gn_done y_set f1a_done f1b_done gelu_a gelu_b f2_done z_set")
        z_turned, ln_stats_set, ln_aggr, ln_veps, ln_rs, norm_set, h_turned, ht_set, scaled_set, ha_set = several(
            sem, "z_turned ln_stats_set ln_aggr ln_veps ln_rs norm_set h_turned ht_set scaled_set ha_set")
        a_loaded, mix_loaded, feed_loaded, finish_loaded = several(
            sem, "a_loaded mix_loaded feed_loaded finish_loaded")
        result_set = sem("result_set")
        (z_tok_set, ln_off_set, weights_set, h_rounded, h_rest, a_rounded, b_rounded,
         b_set, f1_rounded, f1_set, ot_parts, y_rounded, y_rest, chunk_rounded) = several(
            sem, "z_tok_set ln_off_set weights_set h_rounded h_rest a_rounded b_rounded "
                 "b_set f1_rounded f1_set ot_parts y_rounded y_rest chunk_rounded")

        class Item:

            def __init__(self, n, layer, count):
                self.n, self.k, self.layer, self.layers, self.count = n, n % NB, layer, layer + 1, count

            last = property(lambda self: self.count(self.n))
            now = property(lambda self: self.count(self.n + 1))
            next = property(lambda self: self.count(self.n + 1 + NB))

        def slots(eng, numbers, slot, turn=None):
            counts = {}

            def count(items):
                if items not in counts:
                    counts[items] = items if turn is None else eng.snap(NB * turn + items)
                return counts[items]

            def at(j):
                if turn is None and not 0 <= j < ITEMS:
                    return None
                return Item(j, j // NB if turn is None else turn + j // NB, count)

            for n in numbers:
                slot(n, at)

        def full_slots(eng, slot):
            with eng.Fori(0, L - 1) as turn:
                slots(eng, range(3, 3 + NB), slot, turn)
            slots(eng, range(ITEMS - NB + 3, ITEMS + 3), slot)

        def last_layer(item):
            return isinstance(item.layer, int) and item.layer == L - 1

        turn_bank, fold_bank, in_bank = (X1, X2, Z2, Z2), (X3, M1, Z2, Z2), (Y1, Y2) * 2 + (X1, X2) * 2
        block = ctx.enter_context(nc.Block())

        @block.sync
        def _(sp):
            by_chunk = "(c p) d -> p c d"

            def load_x(k):
                sp.dma_start(x_in[:, k], x[k].rearrange(by_chunk, p=P)).then_inc(x_loaded[k], 16)

            sp.dma_start(const[:, :], constants).then_inc(consts_in, 16)
            load_x(0)
            sp.dma_start(kqv_raw[:, :, :], Wkqv.rearrange("l p n -> p l n")).then_inc(kqv_in, 16)
            load_x(1)
            sp.dma_start(wm1_raw[:, :, :], Wm1.rearrange("l p n -> p l n")).then_inc(wm1_in, 16)
            sp.dma_start(gate_rows[:, :], Wg).then_inc(gate_in, 16)
            load_x(2)
            load_x(3)
            first = 0
            for source, halves in ((bm1, 2), (bm2, 1), (gn_g, 1), (gn_b, 1), (bf1, 2), (bf2, 1), (ln_g, 1), (ln_b, 1)):
                for h in range(halves):
                    sp.dma_start(rows[first:first + L, :], source[:, h * D:(h + 1) * D]).then_inc(rows_in, 16)
                    first += L
            sp.dma_start(wm2_raw[:, :, :], Wm2.rearrange("l p n -> p l n")).then_inc(wm2_in, 16)
            for k in range(4, NB):
                load_x(k)
            sp.dma_start(wf1_raw[:, :, :], Wf1.rearrange("l p n -> p l n")).then_inc(wf_in, 16)
            sp.dma_start(wf2_raw[:, :, :, :], Wf2.rearrange("l (h p) n -> p l h n", h=2)).then_inc(wf_in, 16)
            sp.dma_start(expert_rows[:, :, :], We.rearrange("e o d -> o e d")).then_inc(experts_in, 16)
            sp.wait_ge(ones_set, 1)
            for j in range(P // E):
                sp.dma_start(expert_b[E * j:E * j + E, j % C], be).then_inc(be_in, 16)
            sp.dma_start(ln_bc[:, 0], ln_g.partition_broadcast(P)).then_inc(bc_in, 16)
            sp.dma_start(ln_bc[:, 1], ln_b.partition_broadcast(P)).then_inc(bc_in, 16)
            for k in range(NB):
                sp.wait_ge(result_set, k + 1)
                sp.dma_start(out[k].rearrange(by_chunk, p=P), x_in[:, k]).then_inc(stored, 16)
            sp.wait_ge(stored, 16 * NB)

        @block.tensor
        def _(pe):
            def product(dst, weights, moving, rest=None):
                pe.matmul(dst, weights(0), moving(0), start=True, stop=False)
                pe.matmul(dst, weights(1), moving(0), start=False, stop=False)
                if rest:
                    pe.wait_ge(*rest)
                return pe.matmul(dst, weights(0), moving(1), start=False, stop=True)

            def turn_kqv(l):
                if l == 3:
                    pe.wait_ge(folded_set, l)
                for j in range(3):
                    mm = pe.transpose(turn_bank[l][:, j * D:(j + 1) * D], kqv_raw[:, l, j * D:(j + 1) * D], ident)
                mm.then_inc(turned, 1)

            def fold(l):
                pe.wait_ge(turned_set, l + 1)
                bank, w = fold_bank[l], kqv_t[:, l % 2]
                pe.matmul(bank[:, 0:D], w[:, D:2 * D], w[:, 0:D], start=True, stop=True)
                pe.matmul(bank[:, D:3 * D], w[:, 2 * D:], wm1_raw[:, l, :], start=True, stop=True).then_inc(folded, 1)

            def take_in(k, free):
                pe.wait_ge(ha_set, k + 1)
                if free:
                    pe.wait_ge(*free)
                for c in range(C):
                    mm = pe.transpose(in_bank[k][:, c * P:(c + 1) * P], ha[:, k, c, 0:D], ident)
                mm.then_inc(h_turned, 1)

            def ask_gate(k):
                pe.wait_ge(xnt_set, k + 1)
                for c in range(C):
                    i = k * C + c
                    mm = pe.matmul(Z1[:, i * E:(i + 1) * E], xnt[:, i, :], gate_w[:, :], start=True, stop=True)
                if k == NB - 1:
                    mm.then_inc(logits_done, 1)

            def ask_experts(chunk, free=None):
                pe.wait_ge(chunk_set, chunk.now)
                for h, (bank, done) in enumerate(((X1, experts_a), (X2, experts_b))):
                    if h and free:
                        pe.wait_ge(*free)
                    product(bank[:, :], lambda part: chunk_t[:, chunk.k % 2, part, :],
                            lambda part: expert_w[:, part, h * HALF * D:(h + 1) * HALF * D]).then_inc(done, 1)

            def bias_weights():
                pe.wait_ge(route_set, 1)
                for batch in range(2):
                    mm = pe.transpose(X1[:, batch * P:(batch + 1) * P],
                                      route[:, batch * RC:(batch + 1) * RC, :].rearrange("p c e -> p (c e)"), ident)
                mm.then_inc(route_turned, 1)

            def route_biases(k):
                batch, j = divmod(k, BATCH)
                of = slice(j * CE, (j + 1) * CE)
                pe.matmul(Z2[:, :], route_t[of, batch, :], expert_b[of, :, :].rearrange("p c d -> p (c d)"),
                          start=True, stop=True).then_inc(bias_done, 1)

            pe.wait_ge(consts_in, 16)
            pe.wait_ge(kqv_in, 16)
            turn_kqv(0)
            turn_kqv(1)
            pe.wait_ge(wm1_in, 16)
            fold(0)
            pe.wait_ge(gate_in, 16)
            pe.transpose(Z2[:, 0:E], gate_rows[:, :], ident[0:E, 0:E]).then_inc(gate_t, 1)
            take_in(0, None)
            fold(1)
            take_in(1, None)
            pe.wait_ge(gate_set, 1)
            ask_gate(0)
            pe.wait_ge(rows_in, 16 * 10)
            pe.transpose(Z2[:, 0:10 * L], rows[:, :], ident[0:10 * L, 0:10 * L]).then_inc(params_t, 1)
            take_in(2, (xnt_set, 1))
            take_in(3, (xnt_set, 2))
            pe.wait_ge(folded_set, 2)
            pe.wait_ge(params_set, 1)

            def ask_gates(sequences):
                for k in sequences:
                    ask_gate(k)

            def ask_last_gate():
                ask_gate(NB - 1)
                pe.wait_ge(logits_set, 1)

            meanwhile = {1: lambda: ask_gates(range(2, 5)), 2: ask_last_gate}

            def attend(k, c):
                dst = o_sums[:, c // 2, c % 2, 0:D + 1]
                mm = pe.matmul(dst, scores[:, c * P:(c + 1) * P], ha[:, k, c, 0:D + 1], start=True, stop=(c == 0))
                if c:
                    mm = pe.matmul(dst, gt[:, c * P:(c + 1) * P], past[:, c - 1, 0:D + 1], start=False, stop=True)
                return mm

            def slot(n, at):
                mine, mixing, feeding, finishing = at(n), at(n - 1), at(n - 2), at(n - 3)
                if mine:
                    k = mine.k
                    if k == 0:
                        pe.wait_ge(a_loaded, mine.layers)
                    pe.wait_ge(h_rest, mine.now)
                    if finishing:
                        pe.wait_ge(prod_a, finishing.now)
                    product(X1[:, :], lambda part: a_w[:, part, :], lambda part: h_parts[:, part, :]).then_inc(g_done, 1)
                if finishing and last_layer(finishing):
                    route_biases(finishing.k)
                if mixing:
                    pe.wait_ge(o_half, mixing.now)
                    for c in range(C):
                        if c == C // 2:
                            pe.wait_ge(o_set, mixing.now)
                        mm = pe.transpose(Y2[:, c * P:(c + 1) * P], o_tok[:, c, :], ident)
                    mm.then_inc(ot_done, 1)
                if mine:
                    pe.wait_ge(ha_set, mine.now)
                    if finishing:
                        pe.wait_ge(prod_b, finishing.now)
                    for c in range(C - 1):
                        mm = pe.matmul(X2[:, c * AUG:c * AUG + D + 1], ha[:, k, c, 0:D], ha[:, k, c, 0:D + 1],
                                       start=True, stop=True)
                    mm.then_inc(gram_done, 1)
                    pe.wait_ge(gt_set, mine.now)
                    for c in range(C):
                        mm = pe.matmul(X3[:, c * P:(c + 1) * P], ht[:, k, c * P:(c + 1) * P], gt[:, c * P:(c + 1) * P],
                                       start=True, stop=True)
                    mm.then_inc(scores_done, 1)
                if mixing:
                    if mixing.k == 0:
                        pe.wait_ge(mix_loaded, mixing.layers)
                        pe.wait_ge(b_set, mixing.layers)
                    pe.wait_ge(ot_set, mixing.now)
                    if feeding:
                        pe.wait_ge(gn_done, feeding.now)
                    product(Y1[:, :], lambda part: b_w[:, part, 0:D], lambda part: ot[:, part, :],
                            (ot_parts, mixing.now)).then_inc(a_done, 1)
                    product(Y2[:, :], lambda part: b_w[:, part, D:], lambda part: ot[:, part, :]).then_inc(gate_done, 1)
                if n in meanwhile:
                    meanwhile[n]()
                if feeding and n > 2:
                    if not mine:
                        pe.wait_ge(prod_a, finishing.now)
                    ask_experts(feeding, (past_set, mine.now) if mine else (prod_b, finishing.now))
                if feeding:
                    if feeding.k == 0:
                        pe.wait_ge(feed_loaded, feeding.layers)
                        pe.wait_ge(f1_set, feeding.layers)
                    if finishing and last_layer(finishing):
                        pe.wait_ge(bias_set, finishing.k + 1)
                    pe.wait_ge(y_rounded, feeding.now)
                    rounded, rest = y_parts[:, 0, :], y_parts[:, 1, :]
                    pe.matmul(Z2[:, :], f1_w[:, 0, D:], rounded, start=True, stop=False)
                    pe.matmul(Z2[:, :], f1_w[:, 1, D:], rounded, start=False, stop=False)
                    if finishing:
                        pe.wait_ge(z_tok_set, finishing.now)
                    pe.matmul(Z1[:, :], f1_w[:, 0, 0:D], rounded, start=True, stop=False)
                    pe.matmul(Z1[:, :], f1_w[:, 1, 0:D], rounded, start=False, stop=False)
                    pe.wait_ge(y_rest, feeding.now)
                    pe.matmul(Z2[:, :], f1_w[:, 0, D:], rest, start=False, stop=True).then_inc(f1b_done, 1)
                    pe.matmul(Z1[:, :], f1_w[:, 0, 0:D], rest, start=False, stop=True).then_inc(f1a_done, 1)
                if mine:
                    pe.wait_ge(past_set, mine.now)
                    pe.wait_ge(scores_set, mine.now)
                    attend(k, 0)
                if mixing:
                    pe.wait_ge(mixed_set, mixing.now)
                    pe.matmul(Y1[:, :], w2_w[:, :], mixed[:, :], start=True, stop=True).then_inc(mixed_done, 1)
                if feeding:
                    pe.wait_ge(gelu_b, feeding.now)
                    pe.matmul(Z2[:, :], f2_w[:, 1, :], gelu[:, 1, :], start=True, stop=False)
                    pe.wait_ge(gelu_a, feeding.now)
                    pe.matmul(Z2[:, :], f2_w[:, 0, :], gelu[:, 0, :], start=False, stop=True).then_inc(f2_done, 1)
                if mine:
                    attend(k, 1)
                if mixing:
                    pe.wait_ge(gn_means, mixing.now)
                    pe.matmul(Y2[:, 0:1], mean_of[:, :], gn_m[:, :], start=True, stop=True).then_inc(gn_mean, 1)
                if finishing and not last_layer(finishing):
                    pe.wait_ge(norm_set, finishing.now)
                    for c in range(C):
                        mm = pe.transpose(Z1[:, c * P:(c + 1) * P], norm[:, c, :], ident)
                    mm.then_inc(h_turned, 1)
                if mine:
                    attend(k, 2)
                    attend(k, 3).then_inc(o_done, 1)
                if mixing:
                    pe.wait_ge(gn_parts, mixing.now)
                    pe.matmul(Y2[:, 0:1], mean_of[:, :], gn_p[:, :], start=True, stop=True).then_inc(gn_var, 1)
                if feeding:
                    if finishing and not last_layer(finishing):
                        pe.wait_ge(ht_set, finishing.next)
                    pe.wait_ge(z_set, feeding.now)
                    for c in range(C):
                        mm = pe.transpose(Z1[:, c * P:(c + 1) * P], zt[:, c * P:(c + 1) * P], ident)
                    mm.then_inc(z_turned, 1)

            slots(pe, [0], slot)
            take_in(4, (gt_set, 1))
            ask_gate(1)
            pe.wait_ge(xnt_set, 5)
            slots(pe, [1], slot)
            take_in(5, (past_set, 2))
            take_in(6, (gt_set, 2))
            ask_gate(5)
            take_in(7, (xnt_set, 6))
            ask_gate(6)
            pe.wait_ge(xnt_set, NB)
            slots(pe, [2], slot)
            pe.wait_ge(experts_in, 16)
            pe.wait_ge(gt_set, 3)
            pe.wait_ge(past_set, 3)
            for e in range(E):
                mm = pe.transpose((X1, X2)[e // HALF][:, e % HALF * D:(e % HALF + 1) * D], expert_rows[:, e, :], ident)
            mm.then_inc(expert_t, 1)
            turn_kqv(2)
            fold(2)
            turn_kqv(3)
            pe.wait_ge(expert_set, 1)
            bias_weights()
            pe.wait_ge(route_t_set, 1)
            ask_experts(Item(0, 0, int))
            fold(3)
            pe.wait_ge(folded_set, L)
            pe.wait_ge(be_in, 16 * (P // E))
            full_slots(pe, slot)

        @block.scalar
        def _(act):
            def set_kqv(l):
                act.wait_ge(turned, l + 1)
                if l >= 2:
                    act.wait_ge(folded, l - 1)
                act.copy(kqv_t[:, l % 2], turn_bank[l][:, 0:3 * D]).then_inc(turned_set, 1)

            def set_folded(l):
                act.wait_ge(folded, l + 1)
                act.mul(a_all[:, l, :], fold_bank[l][:, 0:D], float(D) ** -0.5)
                act.copy(b_all[:, l, :], fold_bank[l][:, D:3 * D]).then_inc(folded_set, 1)

            def set_xnt(k):
                act.wait_ge(h_turned, k + 1)
                act.copy(ht[:, k, :], in_bank[k][:, :]).then_inc(ht_set, 1)
                act.copy(xnt[:, k * C:(k + 1) * C, :].rearrange("p c t -> p (c t)"), in_bank[k][:, :]).then_inc(xnt_set, 1)

            def stage_chunk(chunk, used=None):
                if used:
                    act.wait_ge(experts_b, used.now)
                    act.wait_ge(prod_b, used.now)
                act.copy(chunk_t[:, chunk.k % 2, 0, :], xnt[:, chunk.last, :]).then_inc(chunk_rounded, 1)
                act.copy(chunk_r[:, chunk.k % 2, :], route[:, chunk.last, :]).then_inc(weights_set, 1)

            def load_a(item):
                act.wait_ge(g_done, item.last)
                act.copy(a_w[:, 0, :], a_all[:, item.layer, :]).then_inc(a_rounded, 1)

            def round_h(item):
                if item.n:
                    act.wait_ge(g_done, item.last)
                act.wait_ge(ht_set, item.now)
                act.copy(h_parts[:, 0, :], ht[:, item.k, :]).then_inc(h_rounded, 1)

            def load_mix(item):
                act.wait_ge(*((gn_parts, item.last) if item.n else (wm2_in, 16)))
                act.copy(b_w[:, 0, :], b_all[:, item.layer, :]).then_inc(b_rounded, 1)
                act.mul(w2_w[:, :], wm2_raw[:, item.layer, :], 0.5)
                act.copy(mix_p[:, :], params[:, MIX, item.layer]).then_inc(mix_loaded, 1)

            def load_feed(item):
                act.wait_ge(*((z_set, item.last) if item.n else (wf_in, 32)))
                act.copy(f1_w[:, 0, :], wf1_raw[:, item.layer, :]).then_inc(f1_rounded, 1)
                act.copy(f2_w[:, :, :], wf2_raw[:, item.layer, :, :])
                act.copy(feed_p[:, :], params[:, FEED, item.layer]).then_inc(feed_loaded, 1)

            def slot(n, at):
                mine, mixing, feeding, finishing = at(n), at(n - 1), at(n - 2), at(n - 3)
                if finishing:
                    act.wait_ge(z_turned, finishing.now)
                    if finishing.n:
                        act.wait_ge(norm_set, finishing.last)
                    act.copy(z_tok[:, :, :].rearrange("p c d -> p (c d)"), Z1[:, :]).then_inc(z_tok_set, 1)
                if mine:
                    act.wait_ge(g_done, mine.now)
                    act.copy(gt[:, :], X1[:, :]).then_inc(gt_set, 1)
                following = at(n + 1)
                if following and following.k == 0:
                    load_a(following)
                if mixing:
                    act.wait_ge(ot_done, mixing.now)
                    act.copy(ot[:, 0, :], Y2[:, :]).then_inc(ot_set, 1)
                if feeding:
                    act.wait_ge(gn_coef, feeding.now)
                    act.activation(gn_out[:, :], Y1[:, :], ACT.Identity, bias=gn_c[:, 0:1],
                                   scale=gn_s[:, 0:1]).then_inc(gn_done, 1)
                    act.wait_ge(y_set, feeding.now)
                    if finishing:
                        act.wait_ge(f1a_done, finishing.now)
                    act.copy(y_parts[:, 0, :], y[:, feeding.k % 2, :]).then_inc(y_rounded, 1)
                if mixing:
                    if mixing.k == 0:
                        act.wait_ge(mix_loaded, mixing.layers)
                    act.wait_ge(a_done, mixing.now)
                    act.activation(a_in[:, :], Y1[:, :], ACT.Identity, bias=mix_p[:, 0:1]).then_inc(a_set, 1)
                    act.wait_ge(gate_done, mixing.now)
                    act.activation(tanh_g[:, :], Y2[:, :], ACT.Tanh, bias=mix_p[:, 2:3], scale=0.5).then_inc(tanh_set, 1)
                if following:
                    round_h(following)
                if feeding:
                    act.wait_ge(f1b_done, feeding.now)
                    act.activation(gelu[:, 1, :], Z2[:, :], ACT.Gelu, bias=feed_p[:, 3:4]).then_inc(gelu_b, 1)
                    act.wait_ge(f1a_done, feeding.now)
                    act.activation(gelu[:, 0, :], Z1[:, :], ACT.Gelu, bias=feed_p[:, 2:3]).then_inc(gelu_a, 1)
                if finishing:
                    act.wait_ge(ln_off_set, finishing.now)
                    if finishing.n:
                        act.wait_ge(scaled_set, finishing.last)
                    for c in range(C):
                        last = act.activation(norm[:, c, :], z_tok[:, c, :], ACT.Identity, bias=ln_off[:, c:c + 1],
                                              scale=ln_rstd[:, c:c + 1])
                    last.then_inc(norm_set, 1)
                if mixing and n > 2:
                    stage_chunk(mixing, finishing)
                if finishing and not last_layer(finishing):
                    k = finishing.k
                    if k == 0:
                        act.wait_ge(finish_loaded, finishing.layers)
                    act.wait_ge(h_turned, finishing.next)
                    act.activation(ht[:, k, :], Z1[:, :], ACT.Identity, bias=finish_p[:, 1:2],
                                   scale=finish_p[:, 0:1]).then_inc(ht_set, 1)
                if mine and mine.k == 0:
                    load_mix(mine)
                if mixing and mixing.k == 0:
                    load_feed(mixing)
                if feeding and feeding.k == 0:
                    if feeding.n:
                        act.wait_ge(ha_set, feeding.count(feeding.n + NB))
                        act.wait_ge(ht_set, feeding.count(feeding.n + NB))
                    else:
                        act.wait_ge(bc_in, 32)
                    act.copy(ln_w[:, :, :], ln_bc[:, :, feeding.layer, :])
                    act.copy(finish_p[:, :], params[:, FINISH, feeding.layer]).then_inc(finish_loaded, 1)

            set_kqv(0)
            set_kqv(1)
            set_folded(0)
            act.wait_ge(gate_t, 1)
            act.copy(gate_w[:, :], Z2[:, 0:E]).then_inc(gate_set, 1)
            set_xnt(0)
            act.wait_ge(folded_set, 1)
            act.copy(a_w[:, 0, :], a_all[:, 0, :]).then_inc(a_rounded, 1)
            round_h(Item(0, 0, int))
            set_folded(1)
            set_xnt(1)
            act.wait_ge(params_t, 1)
            by_layer = Z2[:, 0:10 * L].rearrange("p (j l) -> p j l", l=L)
            act.copy(params[:, 0:HALF_B1G, :], by_layer[:, 0:2, :])
            act.mul(params[:, HALF_B1G, :], by_layer[:, B1G, :], 0.5)
            act.copy(params[:, B2:, :], by_layer[:, 2:, :]).then_inc(params_set, 1)
            act.wait_ge(params_set, 1)
            set_xnt(2)
            set_xnt(3)
            slots(act, [0], slot)
            set_xnt(4)
            slots(act, [1], slot)
            for k in range(5, NB):
                set_xnt(k)
            slots(act, [2], slot)
            act.wait_ge(less_top, 1)
            act.activation(expo[:, :, :], expo[:, :, :], ACT.Exp).then_inc(expo_set, 1)
            act.wait_ge(expert_t, 1)
            for h, half in enumerate((X1, X2)):
                last = act.copy(expert_w[:, 0, h * HALF * D:(h + 1) * HALF * D], half[:, :])
            last.then_inc(expert_rounded, 1)
            set_kqv(2)
            set_folded(2)
            set_kqv(3)
            act.wait_ge(xnt_set, 1)
            act.wait_ge(route_set, 1)
            stage_chunk(Item(0, 0, int))
            stage_chunk(Item(1, 0, int))
            act.wait_ge(route_turned, 1)
            act.copy(route_t[:, :, :].rearrange("p b t -> p (b t)"), X1[:, 0:2 * P]).then_inc(route_t_set, 1)
            set_folded(3)
            act.wait_ge(folded_set, L)
            act.wait_ge(xnt_set, NB)
            full_slots(act, slot)

        @block.vector
        def _(dve):
            dve.memset(ha[:, :, :, D:], 1.0)
            dve.memset(mean_of[:, :], 1.0 / P)
            dve.memset(minus_half[:, :], -0.5)
            dve.memset(expert_b[:, :, :], 0.0).then_inc(ones_set, 1)

            def read_in(k):
                dve.wait_ge(x_loaded[k], 16)
                for c in range(C):
                    last = dve.bn_stats(in_st[:, k, c, :], x_in[:, k, c, :])
                last.then_inc(in_stats, 1)
                dve.wait_ge(in_stats, k + 1)
                for c in range(C):
                    last = dve.bn_aggr(in_mv[:, k, c, :], in_st[:, k, c, :])
                last.then_inc(in_aggr, 1)
                dve.wait_ge(in_aggr, k + 1)
                dve.tensor_scalar(in_v[:, k, :], in_mv[:, k, :, 1], EPS, None, ALU.add).then_inc(in_var, 1)

            def normalise_in(k):
                dve.wait_ge(in_rstd, k + 1)
                for c in range(C):
                    last = dve.tensor_scalar(ha[:, k, c, 0:D], x_in[:, k, c, :], in_mv[:, k, c, 0:1],
                                             in_r[:, k, c:c + 1], ALU.subtract, ALU.mult)
                last.then_inc(ha_set, 1)

            routed = (P, CHUNKS, E)
            preferences = preference.unsqueeze(1).to_broadcast(routed)

            def wide(t):
                return t.unsqueeze(2).to_broadcast(routed)

            def choose(i, values):
                dve.tensor_reduce(best[:, i, :], values[:, :, :], AX.X, ALU.max).then_inc(best_set, 1)
                dve.wait_ge(best_set, i + 1)
                dve.tensor_tensor(ties[:, i], values[:, :, :], wide(best[:, i, :]), ALU.is_ge).then_inc(ties_set, 1)
                if i == 0:
                    dve.tensor_tensor(expo[:, :, :], values[:, :, :], wide(best[:, i, :]),
                                      ALU.subtract).then_inc(less_top, 1)
                dve.wait_ge(ties_set, i + 1)
                dve.tensor_tensor(favour[:, i], ties[:, i], preferences, ALU.mult).then_inc(favour_set, 1)
                dve.wait_ge(favour_set, i + 1)
                dve.tensor_reduce(choice[:, i, :], favour[:, i], AX.X, ALU.max).then_inc(choice_set, 1)
                dve.wait_ge(choice_set, i + 1)
                dve.tensor_tensor(chosen[:, i], preferences, wide(choice[:, i, :]), ALU.is_equal).then_inc(chosen_set, 1)
                dve.wait_ge(chosen_set, i + 1)

            def route_first():
                dve.wait_ge(logits_set, 1)
                choose(0, logits)
                dve.scalar_tensor_tensor(second[:, :, :], chosen[:, 0], -3.0e38, logits[:, :, :],
                                         ALU.mult, ALU.add).then_inc(second_set, 1)

            def route_second():
                dve.wait_ge(second_set, 1)
                choose(1, second)
                dve.tensor_tensor(both[:, :, :], chosen[:, 0], chosen[:, 1], ALU.add).then_inc(both_set, 1)
                dve.wait_ge(both_set, 1)
                dve.wait_ge(expo_set, 1)
                dve.tensor_tensor(share[:, :, :], both[:, :, :], expo[:, :, :], ALU.mult).then_inc(share_set, 1)
                dve.wait_ge(share_set, 1)
                dve.tensor_reduce(total[:, 0, :], share[:, :, :], AX.X, ALU.add).then_inc(total_set, 1)
                dve.wait_ge(total_set, 1)
                dve.reciprocal(total[:, 1, :], total[:, 0, :]).then_inc(inverse_set, 1)
                dve.wait_ge(inverse_set, 1)
                dve.tensor_tensor(route[:, :, :], share[:, :, :], wide(total[:, 1, :]), ALU.mult).then_inc(route_set, 1)

            def read_logits():
                dve.wait_ge(logits_done, 1)
                dve.tensor_copy(logits[:, :, :].rearrange("p c e -> p (c e)"), Z1[:, 0:CHUNKS * E]).then_inc(logits_set, 1)

            def add_biases(k):
                dve.wait_ge(bias_done, k + 1)
                flat = x_in[:, k].rearrange("p c d -> p (c d)")
                dve.tensor_tensor(flat, Z2[:, :], flat, ALU.add).then_inc(bias_set, 1)

            def chunk_rest(chunk):
                dve.wait_ge(chunk_rounded, chunk.now)
                parts = chunk_t[:, chunk.k % 2]
                dve.tensor_tensor(parts[:, 1, :], xnt[:, chunk.last, :], parts[:, 0, :].bitcast(F32),
                                  ALU.subtract).then_inc(chunk_set, 1)

            def y_left(item):
                dve.wait_ge(y_rounded, item.now)
                dve.tensor_tensor(y_parts[:, 1, :], y[:, item.k % 2, :], y_parts[:, 0, :].bitcast(F32),
                                  ALU.subtract).then_inc(y_rest, 1)

            def a_rest(item):
                dve.wait_ge(a_rounded, item.layers)
                dve.tensor_tensor(a_w[:, 1, :], a_all[:, item.layer, :], a_w[:, 0, :].bitcast(F32),
                                  ALU.subtract).then_inc(a_loaded, 1)

            def add_result(item):
                k = item.k
                dve.wait_ge(ha_set, item.next)
                dve.wait_ge(x_added, item.now)
                dve.tensor_tensor(x_in[:, k], ha[:, k, :, 0:D], x_in[:, k], ALU.add).then_inc(result_set, 1)

            def weigh(which, bank, done, chunk):
                dve.wait_ge(done, chunk.now)
                experts = slice(which * HALF, (which + 1) * HALF)
                weights = chunk_r[:, chunk.k % 2, experts].unsqueeze(2).to_broadcast((P, HALF, D))
                dve.tensor_tensor(prod[:, experts, :], bank.rearrange("p (e d) -> p e d", e=HALF), weights,
                                  ALU.mult).then_inc((prod_a, prod_b)[which], 1)

            def slot(n, at):
                mine, mixing, feeding, finishing, finished = (at(n - i) for i in range(5))
                last_y = feeding and finishing and not mixing

                def bias_step():
                    dve.wait_ge(x_added, finishing.last)
                    add_biases(finishing.k)

                def norm_stats():
                    dve.wait_ge(z_tok_set, finishing.now)
                    for c in range(C):
                        last = dve.bn_stats(ln_stats[:, c, :], z_tok[:, c, :])
                    last.then_inc(ln_stats_set, 1)

                if mixing:
                    dve.wait_ge(o_done, mixing.now)
                    dve.tensor_tensor(den[:, 0], o_sums[:, :, :, D], norms, ALU.max).then_inc(den_one, 1)
                    dve.wait_ge(den_one, mixing.now)
                    dve.scalar_tensor_tensor(den[:, 1], o_sums[:, :, :, D], -1.0, den[:, 0],
                                             ALU.mult, ALU.max).then_inc(den_set, 1)
                    dve.wait_ge(den_set, mixing.now)
                    dve.reciprocal(den[:, 2], den[:, 1]).then_inc(inv_set, 1)
                if feeding:
                    dve.wait_ge(gn_var, feeding.now)
                    dve.tensor_scalar(gn_v[:, :], Y2[:, 0:1], EPS, None, ALU.add).then_inc(gn_veps, 1)
                if mixing:
                    dve.wait_ge(inv_set, mixing.now)
                    for b, done in enumerate((o_half, o_set)):
                        dve.tensor_tensor(o_tok[:, 2 * b:2 * b + 2, :], o_sums[:, b, :, 0:D],
                                          den[:, 2, b].unsqueeze(2).to_broadcast((P, 2, D)), ALU.mult).then_inc(done, 1)
                if feeding:
                    if feeding.k == 0:
                        dve.wait_ge(feed_loaded, feeding.layers)
                    dve.wait_ge(gn_rstd, feeding.now)
                    dve.tensor_tensor(gn_s[:, :], gn_r[:, :], feed_p[:, 0:1], ALU.mult).then_inc(gn_scale, 1)
                    dve.wait_ge(gn_scale, feeding.now)
                    dve.scalar_tensor_tensor(gn_c[:, :], gn_b2[:, :], gn_s[:, 0:1], feed_p[:, 1:2],
                                             ALU.mult, ALU.add).then_inc(gn_coef, 1)
                if last_y:
                    bias_step()
                if finishing and not last_y:
                    norm_stats()
                if mixing:
                    if mixing.k == 0:
                        dve.wait_ge(b_rounded, mixing.layers)
                        dve.tensor_tensor(b_w[:, 1, :], b_all[:, mixing.layer, :], b_w[:, 0, :].bitcast(F32),
                                          ALU.subtract).then_inc(b_set, 1)
                    dve.wait_ge(ot_set, mixing.now)
                    dve.tensor_tensor(ot[:, 1, :], Y2[:, :], ot[:, 0, :].bitcast(F32), ALU.subtract).then_inc(ot_parts, 1)
                if feeding:
                    k = feeding.k
                    dve.wait_ge(gn_done, feeding.now)
                    dve.tensor_tensor(y[:, k % 2, :], gn_out[:, :], ht[:, k, :], ALU.add).then_inc(y_set, 1)
                if last_y:
                    norm_stats()
                    y_left(feeding)
                if mine:
                    dve.wait_ge(gram_done, mine.now)
                    dve.tensor_copy(past[:, 0, 0:D + 1], X2[:, 0:D + 1]).then_inc(past_one, 1)
                    dve.wait_ge(past_one, mine.now)
                    dve.tensor_tensor(past[:, 1, 0:D + 1], past[:, 0, 0:D + 1], X2[:, AUG:AUG + D + 1],
                                      ALU.add).then_inc(past_two, 1)
                    dve.wait_ge(past_two, mine.now)
                    dve.tensor_tensor(past[:, 2, 0:D + 1], past[:, 1, 0:D + 1], X2[:, 2 * AUG:2 * AUG + D + 1],
                                      ALU.add).then_inc(past_set, 1)
                if finishing:
                    dve.wait_ge(ones_set, 1)
                    dve.wait_ge(ln_stats_set, finishing.now)
                    for c in range(C):
                        last = dve.bn_aggr(ln_mv[:, c, :], ln_stats[:, c, :])
                    last.then_inc(ln_aggr, 1)
                if feeding and feeding.k == 0:
                    dve.wait_ge(f1_rounded, feeding.layers)
                    dve.tensor_tensor(f1_w[:, 1, :], wf1_raw[:, feeding.layer, :], f1_w[:, 0, :].bitcast(F32),
                                      ALU.subtract).then_inc(f1_set, 1)
                if finishing and mixing and last_layer(finishing):
                    bias_step()
                if mine:
                    dve.wait_ge(scores_done, mine.now)
                    dve.tensor_tensor(scores[:, :].rearrange("p (c i) -> p c i", c=C),
                                      X3.rearrange("p (c i) -> p c i", c=C),
                                      causal.unsqueeze(1).to_broadcast((P, C, P)), ALU.mult).then_inc(scores_set, 1)
                if n in meanwhile:
                    meanwhile[n]()
                if mixing:
                    if mixing.k == 0:
                        dve.wait_ge(mix_loaded, mixing.layers)
                    dve.wait_ge(a_set, mixing.now)
                    dve.wait_ge(tanh_set, mixing.now)
                    dve.scalar_tensor_tensor(gated[:, :], Y2[:, :], mix_p[:, 1:2], a_in[:, :],
                                             ALU.add, ALU.mult).then_inc(gated_set, 1)
                if finishing:
                    dve.wait_ge(ln_aggr, finishing.now)
                    dve.tensor_scalar(ln_var[:, :], ln_mv[:, :, 1], EPS, None, ALU.add).then_inc(ln_veps, 1)
                if finishing and not feeding:
                    bias_step()
                if mixing:
                    dve.wait_ge(gated_set, mixing.now)
                    dve.scalar_tensor_tensor(mixed[:, :], tanh_g[:, :], 1.0, gated[:, :],
                                             ALU.add, ALU.mult).then_inc(mixed_set, 1)
                if n == 2:
                    route_first()
                if finishing:
                    dve.wait_ge(ln_rs, finishing.now)
                    dve.scalar_tensor_tensor(ln_off[:, :], ln_mv[:, :, 0], -1.0, ln_rstd[:, :],
                                             ALU.mult, ALU.mult).then_inc(ln_off_set, 1)
                if finished and last_layer(finished):
                    add_result(finished)
                if mixing:
                    dve.wait_ge(mixed_done, mixing.now)
                    dve.bn_stats(gn_st[:, :], Y1[:, :]).then_inc(gn_stats, 1)
                if feeding and n > 2:
                    dve.wait_ge(four_set, finishing.now)
                    dve.wait_ge(weights_set, feeding.now)
                    weigh(0, X1, experts_a, feeding)
                if mixing:
                    dve.wait_ge(ones_set, 1)
                    dve.wait_ge(gn_stats, mixing.now)
                    dve.bn_aggr(gn_mv[:, :], gn_st[:, :]).then_inc(gn_aggr, 1)
                    dve.wait_ge(gn_aggr, mixing.now)
                    dve.tensor_tensor(gn_m[:, :], gn_mv[:, 0:1], mix_p[:, 3:4], ALU.add).then_inc(gn_means, 1)
                if feeding and n > 2:
                    weigh(1, X2, experts_b, feeding)
                if finishing:
                    x_chunk = x_in[:, :, :, :].rearrange("p k c d -> p (k c) d")[:, finishing.last, :]
                    if last_layer(finishing):
                        dve.wait_ge(bias_set, finishing.k + 1)
                    dve.wait_ge(one_set, finishing.now)
                    dve.tensor_tensor(x_chunk, x_chunk, sum_one[:, :], ALU.add).then_inc(x_added, 1)
                if mixing:
                    dve.wait_ge(gn_mean, mixing.now)
                    dve.wait_ge(gn_means, mixing.now)
                    dve.tensor_scalar(gn_d[:, :], Y2[:, 0:1], -1.0, gn_m[:, 0:1], ALU.mult, ALU.add).then_inc(gn_dev, 1)
                    dve.tensor_scalar(gn_b2[:, :], Y2[:, 0:1], -1.0, mix_p[:, 3:4], ALU.mult, ALU.add)
                    dve.wait_ge(gn_dev, mixing.now)
                    dve.scalar_tensor_tensor(gn_p[:, :], gn_d[:, :], gn_d[:, 0:1], gn_mv[:, 1:2],
                                             ALU.mult, ALU.add).then_inc(gn_parts, 1)
                if feeding:
                    dve.wait_ge(f2_done, feeding.now)
                    dve.scalar_tensor_tensor(zt[:, :], Z2[:, :], feed_p[:, 4:5], y[:, feeding.k % 2, :],
                                             ALU.add, ALU.add).then_inc(z_set, 1)
                if mixing and n > 2:
                    chunk_rest(mixing)
                following = at(n + 1)
                if following and following.k == 0:
                    a_rest(following)

            def take_in(sequences):
                for k in sequences:
                    read_in(k)
                    if k > sequences[0]:
                        normalise_in(k - 1)
                normalise_in(sequences[-1])

            meanwhile = {1: lambda: read_in(5), 2: read_logits}
            take_in(range(4))
            a_rest(Item(0, 0, int))
            slots(dve, [0], slot)
            take_in([4])
            slots(dve, [1], slot)
            normalise_in(5)
            take_in([6, 7])
            slots(dve, [2], slot)
            route_second()
            dve.wait_ge(expert_rounded, 1)
            for h, half in enumerate((X1, X2)):
                cols = slice(h * HALF * D, (h + 1) * HALF * D)
                last = dve.tensor_tensor(expert_w[:, 1, cols], half[:, :], expert_w[:, 0, cols].bitcast(F32), ALU.subtract)
            last.then_inc(expert_set, 1)
            chunk_rest(Item(0, 0, int))
            chunk_rest(Item(1, 0, int))
            dve.wait_ge(weights_set, 1)
            weigh(0, X1, experts_a, Item(0, 0, int))
            weigh(1, X2, experts_b, Item(0, 0, int))
            full_slots(dve, slot)
            final = Item(ITEMS - 1, L - 1, int)
            weights = [ln_w[:, j, :].unsqueeze(1).to_broadcast((P, C, D)) for j in range(2)]
            dve.wait_ge(norm_set, final.now)
            dve.tensor_tensor(scaled[:, :, :], norm[:, :, :], weights[0], ALU.mult).then_inc(scaled_set, 1)
            dve.wait_ge(scaled_set, final.now)
            dve.tensor_tensor(ha[:, final.k, :, 0:D], scaled[:, :, :], weights[1], ALU.add).then_inc(ha_set, 1)
            add_result(final)

        @block.gpsimd
        def _(pool):
            def take_in(sequences):
                for k in sequences:
                    pool.wait_ge(in_var, k + 1)
                    pool.tensor_tensor(in_r[:, k, :], in_v[:, k, :], minus_half[:, :], ALU.pow).then_inc(in_rstd, 1)

            def rest_of_h(item):
                pool.wait_ge(h_rounded, item.now)
                pool.tensor_tensor(h_parts[:, 1, :], ht[:, item.k, :], h_parts[:, 0, :].bitcast(F32),
                                   ALU.subtract).then_inc(h_rest, 1)

            def sum_to_four(finishing):
                pool.wait_ge(prod_a, finishing.now)
                pool.wait_ge(prod_b, finishing.now)
                pool.tensor_tensor(sum_four[:, :, :], prod[:, 0:4, :], prod[:, 4:8, :], ALU.add).then_inc(four_set, 1)

            def sum_to_one(finishing):
                pool.wait_ge(four_set, finishing.now)
                pool.tensor_tensor(sum_two[:, :, :], sum_four[:, 0:2, :], sum_four[:, 2:4, :],
                                   ALU.add).then_inc(two_set, 1)
                pool.wait_ge(two_set, finishing.now)
                if finishing.n:
                    pool.wait_ge(x_added, finishing.last)
                pool.tensor_tensor(sum_one[:, :], sum_two[:, 0, :], sum_two[:, 1, :], ALU.add).then_inc(one_set, 1)

            def norm_factor(finishing):
                pool.wait_ge(ln_veps, finishing.now)
                pool.tensor_tensor(ln_rstd[:, :], ln_var[:, :], minus_half[:, :], ALU.pow).then_inc(ln_rs, 1)

            def slot(n, at):
                following, mixing, feeding, finishing = at(n + 1), at(n - 1), at(n - 2), at(n - 3)
                if finishing and not feeding:
                    sum_to_four(finishing)
                    norm_factor(finishing)
                    sum_to_one(finishing)
                    return
                if feeding:
                    pool.wait_ge(gn_veps, feeding.now)
                    pool.tensor_tensor(gn_r[:, :], gn_v[:, :], minus_half[:, 0:1], ALU.pow).then_inc(gn_rstd, 1)
                if finishing:
                    sum_to_four(finishing)
                    sum_to_one(finishing)
                if mixing and feeding:
                    pool.wait_ge(y_rounded, feeding.now)
                    pool.tensor_tensor(y_parts[:, 1, :], y[:, feeding.k % 2, :], y_parts[:, 0, :].bitcast(F32),
                                       ALU.subtract).then_inc(y_rest, 1)
                if finishing:
                    norm_factor(finishing)
                if following:
                    rest_of_h(following)
                if finishing:
                    k = finishing.k
                    if k == 0:
                        pool.wait_ge(finish_loaded, finishing.layers)
                    pool.wait_ge(norm_set, finishing.now)
                    weights = [ln_w[:, j, :].unsqueeze(1).to_broadcast((P, C, D)) for j in range(2)]
                    pool.tensor_tensor(scaled[:, :, :], norm[:, :, :], weights[0], ALU.mult).then_inc(scaled_set, 1)
                    pool.wait_ge(scaled_set, finishing.now)
                    pool.tensor_tensor(ha[:, k, :, 0:D], scaled[:, :, :], weights[1], ALU.add).then_inc(ha_set, 1)

            pool.wait_ge(ones_set, 1)
            take_in(range(4))
            rest_of_h(Item(0, 0, int))
            slots(pool, [0], slot)
            take_in([4])
            slots(pool, [1], slot)
            take_in(range(5, NB))
            slots(pool, [2], slot)
            full_slots(pool, slot)


_INS = ['x', 'Wkqv', 'Wm1', 'bm1', 'Wm2', 'bm2', 'gn_g', 'gn_b', 'Wf1', 'bf1', 'Wf2', 'bf2', 'ln_g', 'ln_b']
_NAMES = [f"L0_attn_{name}" for name in _INS] + ['L0_ffn_Wg', 'L0_ffn_We', 'L0_ffn_be']


def _constants(tokens, experts):
    import numpy as np

    rank = np.arange(P)
    norm = 1 + np.sqrt(np.arange(tokens, dtype=np.float32))
    preference = np.tile(experts - np.arange(experts), (P, 1))
    return np.concatenate([np.eye(P), rank[:, None] <= rank[None, :], norm.reshape(-1, P).T,
                           preference], 1).astype(np.float32)


def kernel(**inputs):
    import numpy as _np
    import concourse.bacc as _bacc
    from concourse import mybir as _mybir
    from concourse.bass_utils import run_bass_kernel_spmd as _run

    nc = _bacc.Bacc("TRN2", target_bir_lowering=False, num_devices=1)
    x, gate = inputs[_NAMES[0]], inputs['L0_ffn_Wg']
    arrays, args = {}, []
    for name in _NAMES:
        a = _np.ascontiguousarray(inputs[name])
        arrays[f"in_{name}_dram"] = a
        args.append(nc.dram_tensor(f"in_{name}_dram", a.shape, _mybir.dt.from_np(a.dtype), kind="ExternalInput").ap())
    consts = _constants(x.shape[1], gate.shape[0])
    arrays["constants_dram"] = consts
    args.append(nc.dram_tensor("constants_dram", consts.shape, F32, kind="ExternalInput").ap())
    args.append(nc.dram_tensor("out_0_dram", x.shape, F32, kind="ExternalOutput").ap())
    retention_moe(nc, *args)
    r = _run(nc, [arrays], core_ids=[0])
    return r.results[0]["out_0_dram"]
```
